# Optimizing a Trainium2 kernel written in Bass

```python
import numpy as np
import jax
import jax.numpy as jnp

def _softmax(x, axis=-1):
    return jax.nn.softmax(x, axis=axis)

def _gelu(x):
    return jax.nn.gelu(x, approximate=True)

def _silu(x):
    return jax.nn.silu(x)

def _sigmoid(x):
    return jax.nn.sigmoid(x)

def _layernorm(x, axis=-1, eps=1e-05):
    m = jnp.mean(x, axis=axis, keepdims=True)
    v = jnp.var(x, axis=axis, keepdims=True)
    return (x - m) / jnp.sqrt(v + eps)

def _scatter_add(tgt, idx, src, axis=0):
    return tgt.at[idx].add(src)

def _segment_sum(src, seg, n):
    return jax.ops.segment_sum(src, seg, n)
kernel_name = 'mk_gnn_resnorm_d2_gnn_r8_50bbb3'

def setup_inputs(seed: int=0):
    np.random.seed(seed)
    _w = jnp.asarray

    def _rec_inputs():
        import jax
        import jax.numpy as jnp
        _gk = jax.random.key(seed)
        x = -0.0003929 + 0.9999 * jax.random.normal(jax.random.fold_in(_gk, 1), (1250, 512), jnp.float32)
        src = jax.random.randint(jax.random.fold_in(_gk, 2), (20000,), 0, 1250, jnp.int32)
        dst = jnp.minimum((1250 * jax.random.uniform(jax.random.fold_in(_gk, 3), (20000,)) ** 2.0).astype(jnp.int32), 9999)
        _o = jnp.argsort(dst, stable=True)
        src = src[_o]
        dst = dst[_o]
        edge_attr_512 = -8.16379e-05 + 0.999858 * jax.random.normal(jax.random.fold_in(_gk, 12), (20000, 512), jnp.float32)
        return (x, src, dst, edge_attr_512)
    x, src, dst, edge_attr_512 = _rec_inputs()

    def _L0_gnn_setup():
        import jax, jax.numpy as jnp
        import numpy as np
        N_NODES = 4096
        N_EDGES = 32768
        D = 512
        NUM_EXPERTS = 4
        TOP_K = 2
        LAYERS = 2
        key = jax.random.key(seed)
        ks = jax.random.split(key, 8)
        x = jax.random.normal(ks[0], (N_NODES, D), dtype=jnp.float32)
        edge_index = jax.random.randint(ks[1], (2, N_EDGES), 0, N_NODES, dtype=jnp.int64)
        s = 1.0 / np.sqrt(D)
        gate_W = jax.random.uniform(ks[2], (D, NUM_EXPERTS), jnp.float32, -s, s)
        gate_b = jax.random.uniform(ks[3], (NUM_EXPERTS,), jnp.float32, -s, s)
        Wl = jax.random.uniform(ks[4], (NUM_EXPERTS, LAYERS, D, D), jnp.float32, -s, s)
        bl = jax.random.uniform(ks[5], (NUM_EXPERTS, LAYERS, D), jnp.float32, -s, s)
        Wr = jax.random.uniform(ks[6], (NUM_EXPERTS, LAYERS, D, D), jnp.float32, -s, s)
        return {'x': x, 'gate_W': gate_W, 'gate_b': gate_b, 'Wl': Wl, 'bl': bl, 'Wr': Wr, 'edge_index': edge_index}
    _L0_gnn_all = _L0_gnn_setup()
    _L0_gnn_in = {k: v for k, v in _L0_gnn_all.items() if k in ('gate_W', 'gate_b', 'Wl', 'bl', 'Wr')}
    del _L0_gnn_all

    def _L1_gnn_setup():
        import jax, jax.numpy as jnp
        import numpy as np
        N_NODES = 2500
        N_EDGES = 25000
        N_SEG = 16
        EXTENT = 32
        N_PATHS = 64
        OP_SIZE = N_SEG * EXTENT
        key = jax.random.key(seed)
        k1, k2, k3, k4, k5, k6 = jax.random.split(key, 6)
        x_nodes = jax.random.normal(k1, (N_NODES, OP_SIZE), dtype=jnp.float32)
        x_edges = jax.random.normal(k2, (N_EDGES, OP_SIZE), dtype=jnp.float32)
        path_coeffs = jax.random.normal(k3, (N_PATHS,), dtype=jnp.float32)
        src = jax.random.randint(k4, (N_EDGES,), 0, N_NODES, dtype=jnp.int64)
        dst = jax.random.randint(k5, (N_EDGES,), 0, N_NODES, dtype=jnp.int64)
        path_indices = jax.random.randint(k6, (N_PATHS, 3), 0, N_SEG, dtype=jnp.int64)
        return {'x_nodes': x_nodes, 'x_edges': x_edges, 'path_coeffs': path_coeffs, 'src': src, 'dst': dst, 'path_indices': path_indices}
    _L1_gnn_all = _L1_gnn_setup()
    _L1_gnn_in = {k: v for k, v in _L1_gnn_all.items() if k in ('path_coeffs', 'path_indices')}
    del _L1_gnn_all
    return {'x': x, 'src': src, 'dst': dst, 'edge_attr_512': edge_attr_512, 'L0_gnn_gate_W': _L0_gnn_in['gate_W'], 'L0_gnn_gate_b': _L0_gnn_in['gate_b'], 'L0_gnn_Wl': _L0_gnn_in['Wl'], 'L0_gnn_bl': _L0_gnn_in['bl'], 'L0_gnn_Wr': _L0_gnn_in['Wr'], 'L1_gnn_path_coeffs': _L1_gnn_in['path_coeffs'], 'L1_gnn_path_indices': _L1_gnn_in['path_indices']}

def reference(x, src, dst, edge_attr_512, L0_gnn_gate_W, L0_gnn_gate_b, L0_gnn_Wl, L0_gnn_bl, L0_gnn_Wr, L1_gnn_path_coeffs, L1_gnn_path_indices):
    import jax
    import jax.numpy as jnp

    def _L0_gnn_ref(x, gate_W, gate_b, Wl, bl, Wr, edge_index):
        import jax, jax.numpy as jnp
        import numpy as np
        N_NODES = 4096
        N_EDGES = 32768
        D = 512
        NUM_EXPERTS = 4
        TOP_K = 2
        LAYERS = 2
        n = x.shape[0]
        src, dst = (edge_index[0], edge_index[1])
        gates = jax.nn.softmax(x @ gate_W + gate_b, axis=-1)
        top_v, top_i = jax.lax.top_k(gates, TOP_K)
        deg = jax.ops.segment_sum(jnp.ones((src.shape[0],), x.dtype), dst, num_segments=n)
        inv_deg = jnp.where(deg > 0, 1.0 / jnp.maximum(deg, 1.0), 0.0)[:, None]

        def sage_conv(h, W_l, b_l, W_r):
            aggr = jax.ops.segment_sum(h[src], dst, num_segments=n) * inv_deg
            return aggr @ W_l + b_l + h @ W_r
        expert_outs = []
        for e in range(NUM_EXPERTS):
            h = x
            for l in range(LAYERS):
                h = sage_conv(h, Wl[e, l], bl[e, l], Wr[e, l])
                h = jax.nn.relu(h)
            expert_outs.append(h)
        expert_outputs = jnp.stack(expert_outs, axis=1)
        sel = jnp.take_along_axis(expert_outputs, top_i[:, :, None], axis=1)
        out = jnp.sum(sel * top_v[:, :, None], axis=1)
        return out

    def _L1_gnn_ref(x_nodes, x_edges, path_coeffs, src, dst, path_indices):
        import jax, jax.numpy as jnp
        import numpy as np
        N_NODES = 2500
        N_EDGES = 25000
        N_SEG = 16
        EXTENT = 32
        N_PATHS = 64
        OP_SIZE = N_SEG * EXTENT
        n_nodes = x_nodes.shape[0]
        x1 = x_nodes[src].reshape(-1, N_SEG, EXTENT)
        x2 = x_edges.reshape(-1, N_SEG, EXTENT)
        i1, i2, i3 = (path_indices[:, 0], path_indices[:, 1], path_indices[:, 2])
        contrib = path_coeffs[None, :, None] * x1[:, i1, :] * x2[:, i2, :]
        edge_out = jnp.zeros((x2.shape[0], N_SEG, EXTENT), x_nodes.dtype).at[:, i3, :].add(contrib)
        out = jnp.zeros((n_nodes, OP_SIZE), x_nodes.dtype).at[dst].add(edge_out.reshape(-1, OP_SIZE))
        return out
    edge_index = jnp.stack([src, dst])
    x = _layernorm(x + _L0_gnn_ref(x, L0_gnn_gate_W, L0_gnn_gate_b, L0_gnn_Wl, L0_gnn_bl, L0_gnn_Wr, edge_index), axis=-1)
    x = _layernorm(x + _L1_gnn_ref(x, edge_attr_512, L1_gnn_path_coeffs, src, dst, L1_gnn_path_indices), axis=-1)
    return x

_drawn_inputs = setup_inputs


def setup_inputs(seed=0):
    import zlib

    import numpy as np

    out = dict(_drawn_inputs(seed))
    spreads = {}
    factors = {'L0_gnn_gate_b': 4.591, 'L0_gnn_bl': 5.747}
    for name, (base, spread) in spreads.items():
        noise = np.random.default_rng([zlib.crc32(name.encode()), seed]).standard_normal(out[name].shape)
        drawn = base * np.exp(spread * noise) if base else spread * noise
        out[name] = jnp.asarray(drawn.astype(out[name].dtype))
    for name, factor in factors.items():
        out[name] = (out[name] * factor).astype(out[name].dtype)
    return out
```

```python
import concourse.bass as bass
from concourse import mybir
from contextlib import ExitStack

F32 = mybir.dt.float32
BF16 = mybir.dt.bfloat16
FP16 = mybir.dt.float16
I32 = mybir.dt.int32
ALU = mybir.AluOpType
ACT = mybir.ActivationFunctionType
AX = mybir.AxisListType

P = 128
N = 1250
NT = (N + P - 1) // P
NP = NT * P
LAST = N - (NT - 1) * P
D = 512
KT = D // P
NE = 4
E = 20000
EP = 125
ET = E // EP
SEG, EXT, PATHS = 16, 32, 64
BLK = 4
NB = ET // BLK
G = 8
NG = ET // G
PC = 16
NC = PATHS // PC
CW = PC * EXT
SPANS = [(0, 4), (4, 4), (8, 2)]
EPS = 1e-5
AW = 5


class Chain:

    def __init__(self, eng, sem):
        self.eng, self.sem, self.n = eng, sem, 0

    def __call__(self, ins):
        self.n += 1
        ins.then_inc(self.sem, 1)
        self.eng.wait_ge(self.sem, self.n)


def bcast(ap, shape):
    return ap.broadcast_to(shape)


def normalize(nc, step, rows, stats, mv, rstd, act_sem, dve_sem, act_at, dve_at, dve, out):
    for t in range(NT):
        nc.vector.bn_stats(stats[:, t, :], rows[:, t, :])
    step(nc.vector.memset(rstd[:, 0:1], 0.0))
    for t in range(NT):
        nc.vector.bn_aggr(mv[:, t, :], stats[:, t, :])
    step(nc.vector.memset(rstd[:, 0:1], 0.0))
    nc.vector.tensor_scalar(rstd[:, :], mv[:, :, 1], EPS, None, ALU.add).then_inc(dve_sem, 1)
    dve.wait_ge(act_sem, act_at)
    step(nc.vector.reciprocal(rstd[:, :], rstd[:, :]))
    for t in range(NT):
        ins = nc.vector.tensor_scalar(out[:, t, :], rows[:, t, :], mv[:, t, 0:1], rstd[:, t:t + 1],
                                      ALU.subtract, ALU.mult)
    return ins


def experts_block(nc, top, dram, keep):
    ctx = ExitStack()
    with ctx:
        def sb(name, shape, dt=F32):
            return ctx.enter_context(nc.sbuf_tensor(name, shape, dt))

        def sem(name):
            return ctx.enter_context(nc.semaphore(name))

        X = sb("X", [P, NT, D])
        XT = sb("XT", [P, KT, NP])
        AT = sb("AT", [P, NT, NP])
        AGX = sb("AGX", [P, KT, NP])
        H1 = sb("H1", [P, NT, D])
        H1T = sb("H1T", [P, KT, NP])
        AG1 = sb("AG1", [P, KT, 4 * P])
        WL = sb("WL", [P, KT, D])
        WR = sb("WR", [P, KT, D])
        BB = sb("BB", [P, 2, D])
        INV = sb("INV", [P, NP])
        T1 = sb("T1", [P, 2, D])
        T2 = sb("T2", [P, 2, D])
        GW = sb("GW", [P, KT, NE])
        GB = sb("GB", [P, NE])
        GL = sb("GL", [P, NT, NE])
        RANK = sb("RANK", [P, NT, NE])
        GM = sb("GM", [P, NT])
        GX = sb("GX", [P, NT])
        STATS = sb("STATS", [P, NT, 6])
        MV = sb("MV", [P, NT, 2])
        RSTD = sb("RSTD", [P, NT])
        ohs = H1[:, :, :].rearrange("p t d -> p (t d)").bitcast(BF16)[:, 0:BLK * NP].rearrange("p (b n) -> p b n", b=BLK)
        ohd = H1T[:, :, :].rearrange("p t d -> p (t d)").bitcast(BF16)[:, 0:BLK * P].rearrange("p (b n) -> p b n", b=BLK)
        iota16 = WL[:, :, :].rearrange("p t d -> p (t d)").bitcast(FP16)[:, 0:NP]
        iota32 = AGX[:, 0, :].bitcast(I32)
        ge = AGX[:, 1:3, :].rearrange("p t d -> p (t d)").bitcast(BF16)[0:EP, 0:(NT + 1) * ET].rearrange("p (w k) -> p w k", w=NT + 1)
        ind = AGX[:, 3, :].bitcast(BF16)[0:EP, 0:NT * ET].rearrange("p (w k) -> p w k", w=NT)
        deg = T1[:, :, :]
        ones16 = sb("ones16", [P, P], BF16)
        zero16 = sb("zero16", [P, P], BF16)
        ident = sb("ident", [P, P])
        cnt = XT[0:1, 0:2, :].rearrange("p t d -> p (t d)")[:, 0:NT * ET].rearrange("p (w k) -> p w k", w=NT)
        sc = XT[0:1, 2:3, :].rearrange("p t d -> p (t d)")
        degf = AG1[:, :, :].rearrange("p t d -> p (t d)")[:, 0:NP]
        blocks = sb("blocks", [1, 2, NT], I32)
        ps = ctx.enter_context(nc.psum_tensor("ps", [P, 8, D], F32))

        x_loaded, idx_loaded, gate_loaded = sem("x_loaded"), sem("idx_loaded"), sem("gate_loaded")
        weights_loaded, bias_loaded = sem("weights_loaded"), sem("bias_loaded")
        x_zeroed, consts, iota_i = sem("x_zeroed"), sem("consts"), sem("iota_i")
        iota_h, ind_ready, counts_ps = sem("iota_h"), sem("ind_ready"), sem("counts_ps")
        counts_read = sem("counts_read")
        ranges_ready = sem("ranges_ready")
        oh_ready, oh_free = sem("oh_ready"), sem("oh_free")
        window_ps, window_read = sem("window_ps"), sem("window_read")
        tr_ps, tr_read = sem("tr_ps"), sem("tr_read")
        gate_ps, gate_sub, gate_exp, gates_ready = sem("gate_ps"), sem("gate_sub"), sem("gate_exp"), sem("gates_ready")
        inv_ready = sem("inv_ready")
        agg_ps, agg_read = sem("agg_ps"), sem("agg_read")
        dense_ps, dense_read = sem("dense_ps"), sem("dense_read")
        relu_done, y_added = sem("relu_done"), sem("y_added")
        var_ready, std_ready, mid_ready, mid_stored = sem("var_ready"), sem("std_ready"), sem("mid_ready"), sem("mid_stored")
        chain_v, chain_p = sem("chain_v"), sem("chain_p")
        block = ctx.enter_context(nc.Block())

        @block.sync
        def _(sp):
            sp.dma_start(keep["src"][:, :], dram["srcT"]).then_inc(idx_loaded, 16)
            sp.dma_start(keep["dst"][:, :], dram["dstT"]).then_inc(idx_loaded, 16)
            sp.dma_start(keep["path"][:, :], dram["paths"].rearrange("(a n) -> a n", a=1)).then_inc(idx_loaded, 16)
            sp.dma_start(X[:, 0:NT - 1, :], dram["x"][0:(NT - 1) * P, :].rearrange("(t p) d -> p t d", p=P)).then_inc(x_loaded, 16)
            sp.wait_ge(x_zeroed, 1)
            sp.dma_start(X[0:LAST, NT - 1, :], dram["x"][(NT - 1) * P:N, :]).then_inc(x_loaded, 16)
            sp.dma_start(GW[:, :, :], dram["gate_W"].rearrange("(k p) e -> p k e", p=P)).then_inc(gate_loaded, 16)
            sp.dma_start(GB[:, :], dram["gate_b"].partition_broadcast(P)).then_inc(gate_loaded, 16)
            sp.dma_start(keep["coef"][:, :], dram["coeffs"].partition_broadcast(P)).then_inc(gate_loaded, 16)
            sp.wait_ge(window_ps, NT)
            with sp.Fori(0, NE) as e:
                for l in range(2):
                    sp.wait_ge(dense_read, e * (2 * NT) + l * NT + 2)
                    wl = dram["Wl"][bass.ds(e, 1), l, :, :].rearrange("e (k p) o -> p (e k) o", p=P)
                    wr = dram["Wr"][bass.ds(e, 1), l, :, :].rearrange("e (k p) o -> p (e k) o", p=P)
                    sp.dma_start(WL[:, :, :], wl).then_inc(weights_loaded, 16)
                    sp.dma_start(WR[:, :, :], wr).then_inc(weights_loaded, 16)
                    sp.dma_start(BB[:, l, :], dram["bl"][bass.ds(e, 1), l, :].rearrange("e d -> (e d)").partition_broadcast(P)).then_inc(bias_loaded, 16)
            sp.wait_ge(mid_ready, 1)
            sp.dma_start(dram["x_mid"][0:(NT - 1) * P, :].rearrange("(t p) d -> p t d", p=P), H1[:, 0:NT - 1, :]).then_inc(mid_stored, 16)
            sp.dma_start(dram["x_mid"][(NT - 1) * P:N, :], H1[0:LAST, NT - 1, :]).then_inc(mid_stored, 16)
            sp.wait_ge(mid_stored, 32)

        @block.gpsimd
        def _(pool):
            step = Chain(pool, chain_p)
            nc.gpsimd.memset(X[:, NT - 1, :], 0.0).then_inc(x_zeroed, 1)
            nc.gpsimd.iota(iota32, [[1, NP]], base=0, channel_multiplier=0).then_inc(iota_i, 1)
            nc.gpsimd.memset(ones16[:, :], 1.0)
            nc.gpsimd.memset(zero16[:, :], 0.0)
            step(nc.gpsimd.memset(ident[:, :], 0.0))
            nc.gpsimd.affine_select(out=ident[:, :], in_=ident[:, :], compare_op=ALU.not_equal, fill=1.0,
                                    base=0, pattern=[[-1, P]], channel_multiplier=1).then_inc(consts, 1)
            pool.sem_inc(y_added, 2)
            with pool.Fori(0, NE) as e:
                for t in range(NT):
                    pool.wait_ge(relu_done, e * (2 * NT) + NT + t + 3)
                    nc.gpsimd.tensor_tensor(X[:, t, :], X[:, t, :], T2[:, t % 2, :], ALU.add).then_inc(y_added, 1)

        @block.scalar
        def _(act):
            n = 0
            for t0, nt in SPANS:
                for k in range(KT):
                    act.wait_ge(tr_ps, n + 1)
                    if (t0, k) == (0, 0):
                        act.wait_ge(ranges_ready, 1)
                    nc.scalar.copy(XT[:, k, t0 * P:(t0 + nt) * P], ps[:, 2 + n % 2, 0:nt * P]).then_inc(tr_read, 1)
                    n += 1
            act.wait_ge(gate_sub, 1)
            nc.scalar.activation(GL[:, :, :], GL[:, :, :], ACT.Exp).then_inc(gate_exp, 1)
            act.sem_inc(window_read, 1)
            with act.Fori(0, NT) as w:
                act.wait_ge(window_ps, w + 1)
                for b, (t0, nt) in enumerate(SPANS):
                    nc.scalar.copy(AT[:, t0:t0 + nt, bass.ds(w * P, P)], ps[:, b, 0:nt * P].rearrange("p (t n) -> p t n", n=P))
                nc.scalar.copy(degf[:, bass.ds(w * P, P)], ps[:, 2, 2 * P:3 * P]).then_inc(window_read, 1)
            with act.Fori(0, NE) as e:
                for i in range(NT + 2):
                    if i < NT:
                        act.wait_ge(dense_read, e * (2 * NT) + i + 3)
                        nc.scalar.activation(H1[:, i, :], T1[:, i % 2, :], ACT.Relu).then_inc(relu_done, 1)
                    if i >= 2:
                        t = i - 2
                        act.wait_ge(tr_ps, e * NT + len(SPANS) * KT + t + 1)
                        nc.scalar.copy(H1T[:, :, t * P:(t + 1) * P], ps[:, 2 + t % 2, :].rearrange("p (k n) -> p k n", n=P)).then_inc(tr_read, 1)
                for t in range(NT):
                    act.wait_ge(dense_read, e * (2 * NT) + NT + t + 3)
                    act.wait_ge(y_added, e * NT + t + 1)
                    nc.scalar.activation(T2[:, t % 2, :], T1[:, t % 2, :], ACT.Relu, scale=keep["gates"][:, bass.ds(e * NT + t, 1)]).then_inc(relu_done, 1)
            act.wait_ge(var_ready, 1)
            nc.scalar.activation(RSTD[:, :], RSTD[:, :], ACT.Sqrt).then_inc(std_ready, 1)

        @block.vector
        def _(dve):
            step = Chain(dve, chain_v)
            dve.wait_ge(idx_loaded, 48)
            nc.vector.tensor_copy(keep["srcF"][:, :], keep["src"][:, :])
            nc.vector.tensor_scalar(keep["path"][:, :], keep["path"][:, :], EXT, None, ALU.mult)
            step(nc.vector.tensor_scalar(keep["dstF"][:, :], keep["dst"][:, :], -1.0, float(NP), ALU.max, ALU.min))
            for w in range(NT + 1):
                last = nc.vector.tensor_scalar(ge[:, w, :], keep["dstF"][:, :], float(w * P), None, ALU.is_ge)
            step(last)
            nc.vector.tensor_tensor(ind, ge[:, 0:NT, :], ge[:, 1:NT + 1, :], ALU.subtract).then_inc(ind_ready, 1)
            dve.wait_ge(iota_i, 1)
            step(nc.vector.tensor_copy(iota16, iota32))
            dve.wait_ge(counts_ps, 1)
            step(nc.vector.tensor_scalar(cnt.rearrange("p w k -> p (w k)").rearrange("p (b n) -> p b n", b=4), ps[0:1, 4:8, 0:400], 1.0, None, ALU.min))
            step(nc.vector.tensor_copy(keep["present"][:, :, :], cnt))
            asc, bp, gp, s3, m1 = sc[:, 0:64], sc[:, 64:64 + NT * NB], sc[:, 500:500 + NT * NG], sc[:, 720:720 + NT * NB], sc[:, 1130:1150]
            bp3, gp3 = bp.rearrange("p (w k) -> p w k", w=NT), gp.rearrange("p (w g) -> p w g", w=NT)
            step(nc.vector.tensor_copy(asc, iota32[0:1, 0:64]))
            nc.vector.tensor_reduce(bp3, cnt.rearrange("p w (b k) -> p w b k", k=BLK), AX.X, ALU.max)
            step(nc.vector.tensor_reduce(gp3, cnt.rearrange("p w (g k) -> p w g k", k=G), AX.X, ALU.max))

            def first_and_end(flags, size, n, lo, hi):
                s = s3[:, 0:n * size].rearrange("p (n s) -> p n s", n=n)
                r, q = m1[:, 0:n], iotas
                step(nc.vector.tensor_scalar(q[:, 0:size], asc[:, 0:size], -1.0, 100.0, ALU.mult, ALU.add))
                step(nc.vector.tensor_tensor(s, flags, q[:, 0:size].unsqueeze(1).broadcast_to([1, n, size]), ALU.mult))
                step(nc.vector.tensor_reduce(r, s, AX.X, ALU.max))
                step(nc.vector.tensor_scalar(r, r, -1.0, 100.0, ALU.mult, ALU.add))
                step(nc.vector.tensor_scalar(r, r, float(size - 1), None, ALU.min))
                step(nc.vector.tensor_copy(lo, r))
                step(nc.vector.tensor_scalar(r, r, 1.0, None, ALU.add))
                step(nc.vector.tensor_scalar(q[:, 0:size], asc[:, 0:size], 1.0, None, ALU.add))
                step(nc.vector.tensor_tensor(s, flags, q[:, 0:size].unsqueeze(1).broadcast_to([1, n, size]), ALU.mult))
                step(nc.vector.tensor_reduce(m2[:, 0:n], s, AX.X, ALU.max))
                step(nc.vector.tensor_tensor(r, r, m2[:, 0:n], ALU.max))
                step(nc.vector.tensor_copy(hi, r))

            iotas, m2 = sc[:, 1160:1210], sc[:, 1220:1240]
            first_and_end(bp3, NB, NT, blocks[:, 0, :], blocks[:, 1, :])
            first_and_end(gp3.rearrange("p w g -> p g w"), NT, NG, keep["windows"][:, 0, 1:NG + 1], keep["windows"][:, 1, 1:NG + 1])
            nc.vector.memset(m2, 0.0).then_inc(ranges_ready, 1)
            dve.wait_ge(gate_loaded, 48)
            dve.wait_ge(gate_ps, 1)
            step(nc.vector.tensor_tensor(GL[:, :, :], ps[:, 3, 0:NT * NE].rearrange("p (t e) -> p t e", e=NE), GB[:, :].unsqueeze(1).broadcast_to([P, NT, NE]), ALU.add))
            step(nc.vector.tensor_reduce(GM[:, :], GL[:, :, :], AX.X, ALU.max))
            nc.vector.tensor_tensor(GL[:, :, :], GL[:, :, :], GM[:, :].unsqueeze(2).broadcast_to([P, NT, NE]), ALU.subtract).then_inc(gate_sub, 1)
            dve.wait_ge(gate_exp, 1)
            step(nc.vector.tensor_reduce(GM[:, :], GL[:, :, :], AX.X, ALU.add))
            step(nc.vector.reciprocal(GM[:, :], GM[:, :]))
            step(nc.vector.tensor_tensor(GL[:, :, :], GL[:, :, :], GM[:, :].unsqueeze(2).broadcast_to([P, NT, NE]), ALU.mult))
            step(nc.vector.memset(RANK[:, :, :], 0.0))
            for a in range(NE):
                for b in range(a + 1, NE):
                    step(nc.vector.tensor_tensor(GX[:, :], GL[:, :, b], GL[:, :, a], ALU.is_gt))
                    nc.vector.tensor_tensor(RANK[:, :, a], RANK[:, :, a], GX[:, :], ALU.add)
                    step(nc.vector.tensor_tensor(RANK[:, :, b], RANK[:, :, b], GX[:, :], ALU.subtract))
                    step(nc.vector.tensor_scalar(RANK[:, :, b], RANK[:, :, b], 1.0, None, ALU.add))
            step(nc.vector.tensor_scalar(RANK[:, :, :], RANK[:, :, :], 1.5, None, ALU.is_lt))
            nc.vector.tensor_tensor(keep["gates"][:, :].rearrange("p (e t) -> p t e", e=NE), GL[:, :, :], RANK[:, :, :], ALU.mult).then_inc(gates_ready, 1)
            done = dve.alloc_register("oh_blocks")
            dve.reg_mov(done, 0)
            with dve.Fori(0, NT) as w:
                lo = dve.value_load(blocks[0:1, 0, bass.ds(w, 1)], min_val=0, max_val=NB - 1)
                hi = dve.value_load(blocks[0:1, 1, bass.ds(w, 1)], min_val=1, max_val=NB)
                with dve.Fori(lo, hi) as b:
                    at = dve.snap(done, min_val=0, max_val=NT * NB)
                    for j in range(BLK):
                        dve.wait_ge(oh_free, at * BLK + j + 1)
                        nc.vector.tensor_scalar(ohs[0:EP, j, :], iota16[0:EP, :], keep["srcF"][:, bass.ds(b * BLK + j, 1)], None, ALU.is_equal)
                        nc.vector.tensor_scalar(ohd[0:EP, j, :], iota16[0:EP, bass.ds(w * P, P)], keep["dstF"][:, bass.ds(b * BLK + j, 1)], None, ALU.is_equal).then_inc(oh_ready, 1)
                    dve.reg_add(done, done, 1)
            dve.wait_ge(window_read, NT + 1)
            step(nc.vector.tensor_scalar(INV[:, :], degf, 1.0, None, ALU.max))
            step(nc.vector.reciprocal(INV[:, :], INV[:, :]))
            step(nc.vector.tensor_scalar(degf, degf, 1.0, None, ALU.min))
            step(nc.vector.tensor_tensor(INV[:, :], INV[:, :], degf, ALU.mult))
            n = 0
            for t0, nt in SPANS:
                for k in range(KT):
                    dve.wait_ge(agg_ps, n + 1)
                    nc.vector.tensor_tensor(AGX[:, k, t0 * P:(t0 + nt) * P], ps[:, 4 + n % 4, 0:nt * P], INV[:, t0 * P:(t0 + nt) * P], ALU.mult).then_inc(agg_read, 1)
                    n += 1
            dve.sem_inc(dense_read, 2)
            dve.sem_inc(relu_done, 2)
            with dve.Fori(0, NE) as e:
                def biased(l, t):
                    dve.wait_ge(dense_ps, e * (2 * NT) + l * NT + t + 1)
                    if t == 0:
                        dve.wait_ge(bias_loaded, e * 32 + 16 * (l + 1))
                    dve.wait_ge(relu_done, e * (2 * NT) + l * NT + t + 1)
                    nc.vector.tensor_tensor(T1[:, t % 2, :], ps[:, t % 2, :], BB[:, l, :], ALU.add).then_inc(dense_read, 1)

                for t in range(NT):
                    biased(0, t)
                n = 0
                for t0, nt in SPANS:
                    for k in range(KT):
                        dve.wait_ge(agg_ps, (e + 1) * (len(SPANS) * KT) + n + 1)
                        nc.vector.tensor_tensor(AG1[:, k, 0:nt * P], ps[:, 4 + n % 4, 0:nt * P], INV[:, t0 * P:(t0 + nt) * P], ALU.mult).then_inc(agg_read, 1)
                        n += 1
                    for t in range(t0, t0 + nt):
                        biased(1, t)
            dve.wait_ge(y_added, NE * NT + 2)
            normalize(nc, step, X, STATS, MV, RSTD, std_ready, var_ready, 1, 1, dve, H1).then_inc(mid_ready, 1)

        @block.tensor
        def _(pe):
            pe.wait_ge(consts, 1)
            pe.wait_ge(ind_ready, 1)
            for b in range(4):
                mm = nc.tensor.matmul(ps[0:1, 4 + b, 0:400], ones16[0:EP, 0:1], ind.rearrange("p w k -> p (w k)")[:, b * 400:(b + 1) * 400], start=True, stop=True)
            mm.then_inc(counts_ps, 1)
            pe.wait_ge(x_loaded, 32)
            n = 0
            for t0, nt in SPANS:
                for k in range(KT):
                    if n >= 2:
                        pe.wait_ge(tr_read, n - 1)
                    for t in range(nt):
                        mm = nc.tensor.transpose(ps[:, 2 + n % 2, t * P:(t + 1) * P], X[:, t0 + t, k * P:(k + 1) * P], ident[:, :])
                    mm.then_inc(tr_ps, 1)
                    n += 1
            pe.wait_ge(tr_read, n)
            pe.wait_ge(gate_loaded, 48)
            for t in range(NT):
                for k in range(KT):
                    mm = nc.tensor.matmul(ps[:, 3, t * NE:(t + 1) * NE], XT[:, k, t * P:(t + 1) * P], GW[:, k, :], start=(k == 0), stop=(k == KT - 1))
            mm.then_inc(gate_ps, 1)
            pe.wait_ge(ranges_ready, 1)
            pe.sem_inc(oh_free, BLK)
            done = pe.alloc_register("oh_blocks_pe")
            pe.reg_mov(done, 0)
            with pe.Fori(0, NT) as w:
                lo = pe.value_load(blocks[0:1, 0, bass.ds(w, 1)], min_val=0, max_val=NB - 1)
                hi = pe.value_load(blocks[0:1, 1, bass.ds(w, 1)], min_val=1, max_val=NB)
                pe.wait_ge(window_read, w + 1)
                for b, width in enumerate((4 * P, 4 * P, 3 * P)):
                    nc.tensor.matmul(ps[:, b, 0:width], zero16[:, :], iota16[:, 0:width].bitcast(BF16), start=True, stop=False)
                with pe.Fori(lo, hi) as blk:
                    at = pe.snap(done, min_val=0, max_val=NT * NB)
                    for j in range(BLK):
                        pe.wait_ge(oh_ready, at * BLK + j + 1)
                        for s in range(NT):
                            nc.tensor.matmul(ps[:, s // 4, (s % 4) * P:(s % 4 + 1) * P], ohs[0:EP, j, s * P:(s + 1) * P], ohd[0:EP, j, :], start=False, stop=False, skip_group_check=True)
                        nc.tensor.matmul(ps[:, 2, 2 * P:3 * P], ones16[0:EP, :], ohd[0:EP, j, :], start=False, stop=False, skip_group_check=True).then_inc(oh_free, 1)
                    pe.reg_add(done, done, 1)
                for b, width in enumerate((4 * P, 4 * P, 3 * P)):
                    mm = nc.tensor.matmul(ps[:, b, 0:width], zero16[:, :], iota16[:, 0:width].bitcast(BF16), start=False, stop=True)
                mm.then_inc(window_ps, 1)
            pe.wait_ge(window_read, NT + 1)

            def aggregate(rows, t0, nt, n, before):
                for k in range(KT):
                    before(n + k)
                    for s in range(NT):
                        mm = nc.tensor.matmul(ps[:, 4 + (n + k) % 4, 0:nt * P], rows[:, s, k * P:(k + 1) * P], AT[:, s, t0 * P:(t0 + nt) * P], start=(s == 0), stop=(s == NT - 1))
                    mm.then_inc(agg_ps, 1)

            n = 0
            for t0, nt in SPANS:
                aggregate(X, t0, nt, n, lambda m: pe.wait_ge(agg_read, m - 3) if m >= 4 else None)
                n += KT
            pe.wait_ge(agg_read, n)
            with pe.Fori(0, NE) as e:
                def transposed(t):
                    pe.wait_ge(relu_done, e * (2 * NT) + t + 3)
                    pe.wait_ge(tr_read, e * NT + len(SPANS) * KT + t - 1)
                    for k in range(KT):
                        mm = nc.tensor.transpose(ps[:, 2 + t % 2, k * P:(k + 1) * P], H1[:, t, k * P:(k + 1) * P], ident[:, :])
                    mm.then_inc(tr_ps, 1)

                def dense(l, t, agg, own, at):
                    if t == 0:
                        pe.wait_ge(weights_loaded, e * 64 + 32 * (l + 1))
                    pe.wait_ge(dense_read, e * (2 * NT) + l * NT + t + 1)
                    for k in range(KT):
                        nc.tensor.matmul(ps[:, t % 2, :], agg[:, k, at * P:(at + 1) * P], WL[:, k, :], start=(k == 0), stop=False)
                    for k in range(KT):
                        mm = nc.tensor.matmul(ps[:, t % 2, :], own[:, k, t * P:(t + 1) * P], WR[:, k, :], start=False, stop=(k == KT - 1))
                    mm.then_inc(dense_ps, 1)

                for i in range(NT + 1):
                    if i < NT:
                        dense(0, i, AGX, XT, i)
                    if i >= 1:
                        transposed(i - 1)
                pe.wait_ge(tr_read, (e + 1) * NT + len(SPANS) * KT)
                n = 0
                for t0, nt in SPANS:
                    aggregate(H1, t0, nt, n, lambda m: pe.wait_ge(agg_read, (e + 1) * (len(SPANS) * KT) + m - 3))
                    n += KT
                    pe.wait_ge(agg_read, (e + 1) * (len(SPANS) * KT) + n)
                    for t in range(t0, t0 + nt):
                        dense(1, t, AG1, H1T, t - t0)


def messages_block(nc, top, dram, keep):
    ctx = ExitStack()
    with ctx:
        def sb(name, shape, dt=F32):
            return ctx.enter_context(nc.sbuf_tensor(name, shape, dt))

        def sem(name):
            return ctx.enter_context(nc.semaphore(name))

        SUM = sb("SUM", [P, NT, PATHS * EXT])
        X1 = sb("X1", [P, 2, G, D])
        X2 = sb("X2", [P, 2, G, D])
        PR = sb("PR", [P, 2, G, CW])
        DIF = sb("DIF", [P, 2, G, P], FP16)
        SQ = sb("SQ", [P, G, P])
        S = sb("S", [P, 2, G, P])
        IDX = sb("IDX", [P, 2, G], I32)
        iota_i = sb("iota_i", [P, P], I32)
        iota_f = sb("iota_f", [P, P])
        wbase = sb("wbase", [P, NT])
        zero16 = sb("zero16b", [P, P], BF16)
        zrow16 = sb("zrow16b", [P, CW], BF16)
        STATS = sb("STATSb", [P, NT, 6])
        MV = sb("MVb", [P, NT, 2])
        RSTD = sb("RSTDb", [P, NT])
        ROW = X1[:, :, :, :].rearrange("p a g d -> p (a g) d")[:, 0:NT, :]
        RES = X2[:, :, :, :].rearrange("p a g d -> p (a g) d")[:, 0:NT, :]
        OUT = PR[:, :, :, :].rearrange("p a g d -> p (a g) d")[:, 0:NT, :]
        ps = ctx.enter_context(nc.psum_tensor("psb", [P, 8, D], F32))

        x2_loaded = [sem(f"x2_loaded{i}") for i in range(2)]
        x1_loaded = [sem(f"x1_loaded{i}") for i in range(2)]
        group_used, idx_ready, waited = sem("group_used"), sem("idx_ready"), sem("waited")
        consts, iota_sem, zeroed = sem("constsb"), sem("iota_semb"), sem("zeroed")
        dif_ready, dif_used = sem("dif_ready"), sem("dif_used")
        products_ready, products_used = sem("products_ready"), sem("products_used")
        sq_done = sem("sq_done")
        onehot_ready, sums_ps, sums_read = sem("onehot_ready"), sem("sums_ps"), sem("sums_read")
        res_loaded, var_ready, std_ready, out_ready, out_stored = sem("res_loaded"), sem("var_readyb"), sem("std_readyb"), sem("out_ready"), sem("out_stored")
        chain_v = sem("chain_vb")
        block = ctx.enter_context(nc.Block())

        def windows_of(eng, slot):
            lo = eng.value_load(keep["windows"][0:1, 0, bass.ds(slot, 1)], min_val=0, max_val=NT - 1)
            hi = eng.value_load(keep["windows"][0:1, 1, bass.ds(slot, 1)], min_val=1, max_val=NT)
            return lo, hi

        def groups(eng, body):
            with eng.Fori(0, NG // 2) as turn:
                for half in range(2):
                    body(turn * 2 + half, half, turn)

        @block.sync
        def _(sp):
            def load(g, half, turn):
                sp.wait_ge(group_used, g + 1)
                sp.dma_start(X2[0:EP, half, :, :], dram["edge_attr"][bass.ds(g * (G * EP), G * EP), :].rearrange("(g p) d -> p g d", p=EP)).then_inc(x2_loaded[half], 16)
            groups(sp, load)
            sp.wait_ge(group_used, NG + 2)
            sp.dma_start(RES[:, 0:NT - 1, :], dram["x_mid"][0:(NT - 1) * P, :].rearrange("(t p) d -> p t d", p=P)).then_inc(res_loaded, 16)
            sp.dma_start(RES[0:LAST, NT - 1, :], dram["x_mid"][(NT - 1) * P:N, :]).then_inc(res_loaded, 16)
            sp.wait_ge(out_ready, 1)
            sp.dma_start(dram["out"][0:(NT - 1) * P, :].rearrange("(t p) d -> p t d", p=P), OUT[:, 0:NT - 1, :]).then_inc(out_stored, 16)
            sp.dma_start(dram["out"][(NT - 1) * P:N, :], OUT[0:LAST, NT - 1, :]).then_inc(out_stored, 16)
            sp.wait_ge(out_stored, 32)

        @block.gpsimd
        def _(pool):
            nc.gpsimd.iota(iota_i[:, :], [[1, P]], base=0, channel_multiplier=0).then_inc(iota_sem, 1)
            pool.wait_ge(iota_sem, 1)
            nc.gpsimd.tensor_copy(iota_f[:, :], iota_i[:, :]).then_inc(consts, 1)

            def gather(g, half, turn):
                pool.wait_ge(group_used, g + 1)
                nc.gpsimd.tensor_copy(IDX[0:EP, half, :], keep["src"][:, bass.ds(g * G, G)]).then_inc(idx_ready, 1)
                pool.wait_ge(idx_ready, g + 1)
                pool.sem_inc(waited, 1)
                for j in range(G):
                    nc.gpsimd.indirect_dma_start(out=X1[0:EP, half, j, :], out_offset=None, in_=dram["x_mid"],
                                                 in_offset=bass.IndirectOffsetOnAxis(ap=IDX[0:EP, half, j:j + 1], axis=0)).then_inc(x1_loaded[half], 16)
            groups(pool, gather)

        @block.vector
        def _(dve):
            step = Chain(dve, chain_v)
            nc.vector.memset(SUM[:, :, :], 0.0)
            for w in range(NT):
                nc.vector.memset(wbase[:, w:w + 1], float(w * P))
            nc.vector.memset(zero16[:, :], 0.0)
            step(nc.vector.memset(zrow16[:, :], 0.0))
            for credit in (group_used, dif_used, products_used, sums_ps, sums_read):
                dve.sem_inc(credit, 2)
            dve.sem_inc(zeroed, 1)
            dve.wait_ge(consts, 1)
            regs = [dve.alloc_register(f"path_off{i}") for i in range(2 * PC)]
            pairs = dve.alloc_register("pairs_v")
            dve.reg_mov(pairs, 0)

            def add_sums(slot, c):
                lo, hi = windows_of(dve, slot)
                with dve.Fori(lo, hi) as w:
                    at = dve.snap(pairs, min_val=0, max_val=NT * NG * NC)
                    dve.wait_ge(sums_ps, at + 3)
                    acc = SUM[:, bass.ds(w, 1), c * CW:(c + 1) * CW]
                    nc.vector.tensor_tensor(acc, acc, ps[:, bass.ds((w % 2) * NC + c, 1), :], ALU.add).then_inc(sums_read, 1)
                    dve.reg_add(pairs, pairs, 1)

            def products(g, half, turn):
                dst = keep["dstF"][:, bass.ds(g * G, G)]
                dve.wait_ge(dif_used, g + 1)
                nc.vector.tensor_tensor(DIF[0:EP, half, :, :], iota_f[0:EP, :].unsqueeze(1).broadcast_to([EP, G, P]), dst.unsqueeze(2).broadcast_to([EP, G, P]), ALU.subtract).then_inc(dif_ready, 1)
                for c in range(NC):
                    dve.load(regs[0:PC], keep["path"][0:1, c * PC:(c + 1) * PC])
                    dve.load(regs[PC:], keep["path"][0:1, PATHS + c * PC:PATHS + (c + 1) * PC])
                    off = [dve.snap(r, min_val=0, max_val=D - EXT) for r in regs]
                    if c == 0:
                        dve.wait_ge(x1_loaded[half], turn * (16 * G) + 16 * G)
                        dve.wait_ge(x2_loaded[half], turn * 16 + 16)
                    dve.wait_ge(products_used, g * NC + c + 1)
                    for j in range(PC):
                        ins = nc.vector.tensor_tensor(PR[0:EP, c % 2, :, j * EXT:(j + 1) * EXT], X1[0:EP, half, :, bass.ds(off[j], EXT)], X2[0:EP, half, :, bass.ds(off[PC + j], EXT)], ALU.mult)
                    ins.then_inc(products_ready, 1)
                    if c >= 1:
                        add_sums(g + 1, c - 1)
                    elif half:
                        add_sums(g, NC - 1)
                    else:
                        with dve.If(turn > 0):
                            add_sums(g, NC - 1)
                dve.drain().then_inc(group_used, 1)

            groups(dve, products)
            add_sums(NG, NC - 1)
            dve.wait_ge(products_used, NG * NC + 2)
            step(nc.vector.memset(ROW, 0.0))
            for c in range(PATHS // (2 * PC)):
                dve.load(regs, keep["path"][0:1, 2 * PATHS + c * 2 * PC:2 * PATHS + (c + 1) * 2 * PC])
                off = [dve.snap(r, min_val=0, max_val=D - EXT) for r in regs]
                for j in range(2 * PC):
                    p = c * 2 * PC + j
                    seg = ROW[:, :, bass.ds(off[j], EXT)]
                    step(nc.vector.scalar_tensor_tensor(seg, SUM[:, :, p * EXT:(p + 1) * EXT], keep["coef"][:, p:p + 1], seg, ALU.mult, ALU.add))
            dve.wait_ge(res_loaded, 32)
            nc.vector.tensor_tensor(ROW[:, 0:NT - 1, :], ROW[:, 0:NT - 1, :], RES[:, 0:NT - 1, :], ALU.add)
            step(nc.vector.tensor_tensor(ROW[0:LAST, NT - 1, :], ROW[0:LAST, NT - 1, :], RES[0:LAST, NT - 1, :], ALU.add))
            normalize(nc, step, ROW, STATS, MV, RSTD, std_ready, var_ready, 1, 1, dve, OUT).then_inc(out_ready, 1)

        @block.scalar
        def _(act):
            made = act.alloc_register("pairs_a")
            act.reg_mov(made, 0)
            act.sem_inc(onehot_ready, 1)
            act.wait_ge(zeroed, 1)

            def onehots(g, half, turn):
                act.wait_ge(dif_ready, g + 1)
                lo, hi = windows_of(act, g + 1)
                for c in range(NC):
                    with act.Fori(lo, hi) as w:
                        at = act.snap(made, min_val=0, max_val=NT * NG * NC)
                        act.wait_ge(onehot_ready, at + 1)
                        nc.scalar.activation(SQ[0:EP, :, :], DIF[0:EP, half, :, :], ACT.Square, bias=wbase[0:EP, bass.ds(w, 1)]).then_inc(sq_done, 1)
                        act.wait_ge(sq_done, at + 1)
                        act.wait_ge(sums_ps, at + 1)
                        nc.scalar.activation(S[0:EP, bass.ds(at % 2, 1), :, :].rearrange("p a g n -> p (a g) n"), SQ[0:EP, :, :], ACT.Relu, bias=1.0, scale=-1.0).then_inc(onehot_ready, 1)
                        act.reg_add(made, made, 1)
                act.drain().then_inc(dif_used, 1)
            groups(act, onehots)
            act.wait_ge(var_ready, 1)
            nc.scalar.activation(RSTD[:, :], RSTD[:, :], ACT.Sqrt).then_inc(std_ready, 1)

        @block.tensor
        def _(pe):
            pe.wait_ge(zeroed, 1)
            pairs = pe.alloc_register("pairs_t")
            pe.reg_mov(pairs, 0)

            def sums(g, half, turn):
                lo, hi = windows_of(pe, g + 1)
                for c in range(NC):
                    with pe.Fori(lo, hi) as w:
                        pe.wait_ge(products_ready, g * NC + c + 1)
                        at = pe.snap(pairs, min_val=0, max_val=NT * NG * NC)
                        pe.wait_ge(onehot_ready, at + 2)
                        pe.wait_ge(sums_read, at + 1)
                        bank = ps[:, bass.ds((w % 2) * NC + c, 1), :].rearrange("p a n -> p (a n)")
                        with pe.If(at % 2 < 1):
                            for j in range(G):
                                mm = nc.tensor.matmul(bank, S[0:EP, 0, j, :], PR[0:EP, c % 2, j, :], start=(j == 0), stop=(j == G - 1))
                            mm.then_inc(sums_ps, 1)
                        with pe.If(at % 2 > 0):
                            for j in range(G):
                                mm = nc.tensor.matmul(bank, S[0:EP, 1, j, :], PR[0:EP, c % 2, j, :], start=(j == 0), stop=(j == G - 1))
                            mm.then_inc(sums_ps, 1)
                        pe.reg_add(pairs, pairs, 1)
                    pe.drain().then_inc(products_used, 1)
            groups(pe, sums)


def gnn_kernel(nc, x, srcT, dstT, edge_attr, gate_W, gate_b, Wl, bl, Wr, coeffs, paths, out):
    ctx = ExitStack()
    with ctx:
        x_mid = nc.dram_tensor("x_mid", (N, D), F32, kind="Internal").ap()
        dram = dict(x=x, srcT=srcT, dstT=dstT, edge_attr=edge_attr, gate_W=gate_W, gate_b=gate_b,
                    Wl=Wl, bl=bl, Wr=Wr, coeffs=coeffs, paths=paths, out=out, x_mid=x_mid)
        keep = {}
        for name, shape, dt in (("src", [EP, ET], I32), ("dst", [EP, ET], I32), ("srcF", [EP, ET], F32),
                                ("dstF", [EP, ET], F32), ("path", [1, 3 * PATHS], I32), ("coef", [P, PATHS], F32),
                                ("gates", [P, NE * NT], F32), ("present", [1, NT, ET], mybir.dt.uint8),
                                ("windows", [1, 2, NG + 1], I32)):
            keep[name] = ctx.enter_context(nc.sbuf_tensor(name + "_kept", shape, dt))
        experts_block(nc, ctx, dram, keep)
        messages_block(nc, ctx, dram, keep)


def kernel(x, src, dst, edge_attr_512, L0_gnn_gate_W, L0_gnn_gate_b, L0_gnn_Wl, L0_gnn_bl, L0_gnn_Wr,
           L1_gnn_path_coeffs, L1_gnn_path_indices):
    import numpy as np
    import concourse.bacc as bacc
    from concourse.bass_utils import run_bass_kernel_spmd

    c = np.ascontiguousarray
    arrays = {
        "x": c(x),
        "srcT": c(np.asarray(src).reshape(ET, EP).T),
        "dstT": c(np.asarray(dst).reshape(ET, EP).T),
        "edge_attr": c(edge_attr_512),
        "gate_W": c(L0_gnn_gate_W), "gate_b": c(L0_gnn_gate_b),
        "Wl": c(L0_gnn_Wl), "bl": c(L0_gnn_bl), "Wr": c(L0_gnn_Wr),
        "coeffs": c(L1_gnn_path_coeffs),
        "paths": c(np.asarray(L1_gnn_path_indices).T).reshape(3 * PATHS),
    }
    nc = bacc.Bacc("TRN2", target_bir_lowering=False, num_devices=1)
    args = [nc.dram_tensor(f"in_{k}", a.shape, mybir.dt.from_np(a.dtype), kind="ExternalInput").ap() for k, a in arrays.items()]
    out = nc.dram_tensor("out_dram", (N, D), F32, kind="ExternalOutput").ap()
    gnn_kernel(nc, *args, out)
    r = run_bass_kernel_spmd(nc, [{f"in_{k}": a for k, a in arrays.items()}], core_ids=[0])
    return r.results[0]["out_dram"]
```

```python
import concourse.bass as bass
from concourse import mybir
from contextlib import ExitStack
from itertools import count

F32 = mybir.dt.float32
F32R = mybir.dt.float32r
BF16 = mybir.dt.bfloat16
FP16 = mybir.dt.float16
I32 = mybir.dt.int32
ALU = mybir.AluOpType
ACT = mybir.ActivationFunctionType
AX = mybir.AxisListType

P = 128
N = 1250
NT = (N + P - 1) // P
NP = NT * P
LAST = N - (NT - 1) * P
D = 512
KT = D // P
NE = 4
E = 20000
EP = 125
ET = E // EP
SEG, EXT, PATHS = 16, 32, 64
BLK = 4
NB = ET // BLK
G = 8
NG = ET // G
PC = 16
NC = PATHS // PC
CW = PC * EXT
SPANS = [(0, 4), (4, 4), (8, 2)]
EPS = 1e-5
EXACT = 2048.0
ZV = 6


class Chain:

    def __init__(self, eng, sem):
        self.eng, self.sem, self.n = eng, sem, 0

    def __call__(self, ins):
        self.n += 1
        ins.then_inc(self.sem, 1)
        self.eng.wait_ge(self.sem, self.n)


def bcast(ap, shape):
    return ap.broadcast_to(shape)


def normalize(nc, step, rows, stats, mv, rstd, act_sem, dve_sem, act_at, dve_at, dve, out):
    for t in range(NT):
        nc.vector.bn_stats(stats[:, t, :], rows[:, t, :])
    step(nc.vector.memset(rstd[:, 0:1], 0.0))
    for t in range(NT):
        nc.vector.bn_aggr(mv[:, t, :], stats[:, t, :])
    step(nc.vector.memset(rstd[:, 0:1], 0.0))
    nc.vector.tensor_scalar(rstd[:, :], mv[:, :, 1], EPS, None, ALU.add).then_inc(dve_sem, 1)
    dve.wait_ge(act_sem, act_at)
    step(nc.vector.reciprocal(rstd[:, :], rstd[:, :]))
    for t in range(NT):
        ins = nc.vector.tensor_scalar(out[:, t, :], rows[:, t, :], mv[:, t, 0:1], rstd[:, t:t + 1],
                                      ALU.subtract, ALU.mult)
    return ins


def experts_block(nc, top, dram, keep):
    ctx = ExitStack()
    with ctx:
        def sb(name, shape, dt=F32):
            return ctx.enter_context(nc.sbuf_tensor(name, shape, dt))

        def sem(name):
            return ctx.enter_context(nc.semaphore(name))

        X = sb("X", [P, NT, D])
        XT = sb("XT", [P, KT, NP])
        AT = sb("AT", [P, NT, NP])
        ATR = AT[:, :, :].bitcast(F32R)
        AGX = sb("AGX", [P, KT, NP])
        HH = sb("HH", [P, NT, D], F32R)
        HL = sb("HL", [P, NT, D], F32R)
        H1T = sb("H1T", [P, KT, 4 * P])
        AG1 = sb("AG1", [P, KT, 4 * P])
        W = sb("W", [P, 2, KT, D])
        WL, WR = W[:, 0, :, :], W[:, 1, :, :]
        BB = sb("BB", [P, 2, D])
        INV = sb("INV", [P, NP])
        T1 = sb("T1", [P, 2, D])
        T2 = sb("T2", [P, 2, D])
        GW = sb("GW", [P, KT, NE])
        GB = sb("GB", [P, NE])
        GL = sb("GL", [P, NT, NE])
        RANK = sb("RANK", [P, NT, NE])
        GM = sb("GM", [P, NT])
        GX = sb("GX", [P, NT])
        STATS = sb("STATS", [P, NT, 6])
        MV = sb("MV", [P, NT, 2])
        RSTD = sb("RSTD", [P, NT])
        wbytes = W[:, :, :, :].rearrange("p a k d -> p (a k d)")
        ohs = wbytes.bitcast(BF16)[:, NP:NP + BLK * NP].rearrange("p (b n) -> p b n", b=BLK)
        ohd = H1T[:, :, :].rearrange("p t d -> p (t d)").bitcast(BF16)[:, 0:BLK * P].rearrange("p (b n) -> p b n", b=BLK)
        iota16 = wbytes.bitcast(FP16)[:, 0:NP]
        iota32 = AGX[:, 0, :].bitcast(I32)
        ge = AGX[:, 1:3, :].rearrange("p t d -> p (t d)").bitcast(BF16)[0:EP, 0:(NT + 1) * ET].rearrange("p (w k) -> p w k", w=NT + 1)
        ind = AGX[:, 3, :].bitcast(BF16)[0:EP, 0:NT * ET].rearrange("p (w k) -> p w k", w=NT)
        deg = T1[:, :, :]
        ones16 = sb("ones16", [P, P], BF16)
        zero16 = sb("zero16", [P, P], BF16)
        ident = sb("ident", [P, P])
        identr = sb("identr", [P, P], F32R)
        maxdeg = sb("maxdeg", [P, 1])
        large = sb("large", [P, 1], I32)
        MID = XT[:, :, :].rearrange("p k n -> p (k n)").rearrange("p (t d) -> p t d", d=D)
        cnt = XT[0:1, 0:2, :].rearrange("p t d -> p (t d)")[:, 0:NT * ET].rearrange("p (w k) -> p w k", w=NT)
        sc = XT[0:1, 2:3, :].rearrange("p t d -> p (t d)")
        degf = AG1[:, :, :].rearrange("p t d -> p (t d)")[:, 0:NP]
        blocks = sb("blocks", [1, 2, NT], I32)
        ps = ctx.enter_context(nc.psum_tensor("ps", [P, 8, D], F32))

        x_loaded, idx_loaded, gate_loaded = sem("x_loaded"), sem("idx_loaded"), sem("gate_loaded")
        weights_loaded, bias_loaded = sem("weights_loaded"), sem("bias_loaded")
        x_zeroed, consts, iota_i = sem("x_zeroed"), sem("consts"), sem("iota_i")
        iota_h, ind_ready, counts_ps = sem("iota_h"), sem("ind_ready"), sem("counts_ps")
        counts_read = sem("counts_read")
        ranges_ready = sem("ranges_ready")
        oh_ready, oh_free = sem("oh_ready"), sem("oh_free")
        window_ps, window_read = sem("window_ps"), sem("window_read")
        tr_ps, tr_read = sem("tr_ps"), sem("tr_read")
        gate_ps, gate_sub, gate_exp, gates_ready = sem("gate_ps"), sem("gate_sub"), sem("gate_exp"), sem("gates_ready")
        high_ready, low_ready, large_ready = sem("high_ready"), sem("low_ready"), sem("large_ready")
        agg_ps, agg_read = sem("agg_ps"), sem("agg_read")
        dense_ps, dense_read = sem("dense_ps"), sem("dense_read")
        relu_done, y_added = sem("relu_done"), sem("y_added")
        var_ready, std_ready, mid_ready, mid_stored = sem("var_ready"), sem("std_ready"), sem("mid_ready"), sem("mid_stored")
        chain_v, chain_p = sem("chain_v"), sem("chain_p")
        block = ctx.enter_context(nc.Block())

        @block.sync
        def _(sp):
            sp.dma_start(keep["src"][:, :], dram["srcT"]).then_inc(idx_loaded, 16)
            sp.dma_start(keep["dst"][:, :], dram["dstT"]).then_inc(idx_loaded, 16)
            sp.dma_start(keep["path"][:, :], dram["paths"].rearrange("(a n) -> a n", a=1)).then_inc(idx_loaded, 16)
            sp.dma_start(X[:, 0:NT - 1, :], dram["x"][0:(NT - 1) * P, :].rearrange("(t p) d -> p t d", p=P)).then_inc(x_loaded, 16)
            sp.wait_ge(x_zeroed, 1)
            sp.dma_start(X[0:LAST, NT - 1, :], dram["x"][(NT - 1) * P:N, :]).then_inc(x_loaded, 16)
            sp.dma_start(GW[:, :, :], dram["gate_W"].rearrange("(k p) e -> p k e", p=P)).then_inc(gate_loaded, 16)
            sp.dma_start(GB[:, :], dram["gate_b"].partition_broadcast(P)).then_inc(gate_loaded, 16)
            sp.dma_start(keep["coef"][:, :], dram["coeffs"].partition_broadcast(P)).then_inc(gate_loaded, 16)
            sp.wait_ge(window_ps, NT)
            with sp.Fori(0, NE) as e:
                for l in range(2):
                    sp.wait_ge(dense_read, e * (2 * NT) + l * NT + 2)
                    wl = dram["Wl"][bass.ds(e, 1), l, :, :].rearrange("e (k p) o -> p (e k) o", p=P)
                    wr = dram["Wr"][bass.ds(e, 1), l, :, :].rearrange("e (k p) o -> p (e k) o", p=P)
                    sp.dma_start(WL[:, :, :], wl).then_inc(weights_loaded, 16)
                    sp.dma_start(WR[:, :, :], wr).then_inc(weights_loaded, 16)
                    sp.dma_start(BB[:, l, :], dram["bl"][bass.ds(e, 1), l, :].rearrange("e d -> (e d)").partition_broadcast(P)).then_inc(bias_loaded, 16)
            sp.wait_ge(mid_ready, 1)
            sp.dma_start(dram["x_mid"].rearrange("(t p) d -> p t d", p=P), MID).then_inc(mid_stored, 16)
            sp.wait_ge(mid_stored, 16)

        @block.gpsimd
        def _(pool):
            step = Chain(pool, chain_p)
            nc.gpsimd.memset(X[:, NT - 1, :], 0.0).then_inc(x_zeroed, 1)
            nc.gpsimd.iota(iota32, [[1, NP]], base=0, channel_multiplier=0).then_inc(iota_i, 1)
            nc.gpsimd.memset(ones16[:, :], 1.0)
            nc.gpsimd.memset(zero16[:, :], 0.0)
            step(nc.gpsimd.memset(ident[:, :], 0.0))
            nc.gpsimd.affine_select(out=ident[:, :], in_=ident[:, :], compare_op=ALU.not_equal, fill=1.0,
                                    base=0, pattern=[[-1, P]], channel_multiplier=1).then_inc(consts, 1)
            pool.sem_inc(y_added, 2)
            with pool.Fori(0, NE) as e:
                for t in range(NT):
                    pool.wait_ge(relu_done, e * (2 * NT) + NT + t + 3)
                    nc.gpsimd.tensor_tensor(X[:, t, :], X[:, t, :], T2[:, t % 2, :], ALU.add).then_inc(y_added, 1)

        @block.scalar
        def _(act):
            n = 0
            for t0, nt in SPANS:
                for k in range(KT):
                    act.wait_ge(tr_ps, n + 1)
                    if (t0, k) == (0, 0):
                        act.wait_ge(ranges_ready, 1)
                    nc.scalar.copy(XT[:, k, t0 * P:(t0 + nt) * P], ps[:, 2 + n % 2, 0:nt * P]).then_inc(tr_read, 1)
                    n += 1
            for t in range(NT):
                last = nc.scalar.copy(HH[:, t, :], X[:, t, :])
            last.then_inc(high_ready, 1)
            act.wait_ge(gate_sub, 1)
            nc.scalar.activation(GL[:, :, :], GL[:, :, :], ACT.Exp).then_inc(gate_exp, 1)
            act.sem_inc(window_read, 1)
            with act.Fori(0, NT) as w:
                act.wait_ge(window_ps, w + 1)
                for b, (t0, nt) in enumerate(SPANS):
                    nc.scalar.copy(AT[:, t0:t0 + nt, bass.ds(w * P, P)], ps[:, b, 0:nt * P].rearrange("p (t n) -> p t n", n=P))
                nc.scalar.copy(degf[:, bass.ds(w * P, P)], ps[:, 2, 2 * P:3 * P]).then_inc(window_read, 1)
            with act.Fori(0, NE) as e:
                def gated(t):
                    act.wait_ge(dense_read, e * (2 * NT) + NT + t + 3)
                    act.wait_ge(y_added, e * NT + t + 1)
                    nc.scalar.activation(T2[:, t % 2, :], T1[:, t % 2, :], ACT.Relu, scale=keep["gates"][:, bass.ds(e * NT + t, 1)]).then_inc(relu_done, 1)

                for t in range(NT):
                    act.wait_ge(dense_read, e * (2 * NT) + t + 3)
                    nc.scalar.activation(HH[:, t, :], T1[:, t % 2, :], ACT.Relu).then_inc(relu_done, 1)
                for t0, nt in SPANS:
                    for t in range(t0, t0 + nt):
                        act.wait_ge(tr_ps, e * NT + len(SPANS) * KT + t + 1)
                        nc.scalar.copy(H1T[:, :, (t - t0) * P:(t - t0 + 1) * P], ps[:, 2 + t % 2, :].rearrange("p (k n) -> p k n", n=P)).then_inc(tr_read, 1)
                    for t in range(t0, t0 + nt):
                        gated(t)
            act.wait_ge(var_ready, 1)
            nc.scalar.activation(RSTD[:, :], RSTD[:, :], ACT.Sqrt).then_inc(std_ready, 1)

        @block.vector
        def _(dve):
            step = Chain(dve, chain_v)
            dve.wait_ge(idx_loaded, 48)
            nc.vector.tensor_copy(keep["srcF"][:, :], keep["src"][:, :])
            nc.vector.tensor_scalar(keep["path"][:, :], keep["path"][:, :], EXT, None, ALU.mult)
            step(nc.vector.tensor_scalar(keep["dstF"][:, :], keep["dst"][:, :], -1.0, float(NP), ALU.max, ALU.min))
            for w in range(NT + 1):
                last = nc.vector.tensor_scalar(ge[:, w, :], keep["dstF"][:, :], float(w * P), None, ALU.is_ge)
            step(last)
            nc.vector.tensor_tensor(ind, ge[:, 0:NT, :], ge[:, 1:NT + 1, :], ALU.subtract).then_inc(ind_ready, 1)
            dve.wait_ge(iota_i, 1)
            dve.wait_ge(consts, 1)
            nc.vector.tensor_copy(identr[:, :], ident[:, :])
            step(nc.vector.tensor_copy(iota16, iota32))
            dve.wait_ge(counts_ps, 1)
            step(nc.vector.tensor_scalar(cnt.rearrange("p w k -> p (w k)").rearrange("p (b n) -> p b n", b=4), ps[0:1, 4:8, 0:400], 1.0, None, ALU.min))
            step(nc.vector.tensor_copy(keep["present"][:, :, :], cnt))
            asc, bp, gp, s3, m1 = sc[:, 0:64], sc[:, 64:64 + NT * NB], sc[:, 500:500 + NT * NG], sc[:, 720:720 + NT * NB], sc[:, 1130:1150]
            bp3, gp3 = bp.rearrange("p (w k) -> p w k", w=NT), gp.rearrange("p (w g) -> p w g", w=NT)
            step(nc.vector.tensor_copy(asc, iota32[0:1, 0:64]))
            nc.vector.tensor_reduce(bp3, cnt.rearrange("p w (b k) -> p w b k", k=BLK), AX.X, ALU.max)
            step(nc.vector.tensor_reduce(gp3, cnt.rearrange("p w (g k) -> p w g k", k=G), AX.X, ALU.max))

            def first_and_end(flags, size, n, lo, hi):
                s = s3[:, 0:n * size].rearrange("p (n s) -> p n s", n=n)
                r, q = m1[:, 0:n], iotas
                step(nc.vector.tensor_scalar(q[:, 0:size], asc[:, 0:size], -1.0, 100.0, ALU.mult, ALU.add))
                step(nc.vector.tensor_tensor(s, flags, q[:, 0:size].unsqueeze(1).broadcast_to([1, n, size]), ALU.mult))
                step(nc.vector.tensor_reduce(r, s, AX.X, ALU.max))
                step(nc.vector.tensor_scalar(r, r, -1.0, 100.0, ALU.mult, ALU.add))
                step(nc.vector.tensor_scalar(r, r, float(size - 1), None, ALU.min))
                step(nc.vector.tensor_copy(lo, r))
                step(nc.vector.tensor_scalar(r, r, 1.0, None, ALU.add))
                step(nc.vector.tensor_scalar(q[:, 0:size], asc[:, 0:size], 1.0, None, ALU.add))
                step(nc.vector.tensor_tensor(s, flags, q[:, 0:size].unsqueeze(1).broadcast_to([1, n, size]), ALU.mult))
                step(nc.vector.tensor_reduce(m2[:, 0:n], s, AX.X, ALU.max))
                step(nc.vector.tensor_tensor(r, r, m2[:, 0:n], ALU.max))
                step(nc.vector.tensor_copy(hi, r))

            iotas, m2 = sc[:, 1160:1210], sc[:, 1220:1240]
            first_and_end(bp3, NB, NT, blocks[:, 0, :], blocks[:, 1, :])
            first_and_end(gp3.rearrange("p w g -> p g w"), NT, NG, keep["windows"][:, :, 0], keep["windows"][:, :, 1])
            nc.vector.memset(m2, 0.0).then_inc(ranges_ready, 1)
            dve.wait_ge(high_ready, 1)
            nc.vector.tensor_tensor(HL[:, :, :], X[:, :, :], HH[:, :, :].bitcast(F32), ALU.subtract).then_inc(low_ready, 1)
            dve.wait_ge(gate_loaded, 48)
            dve.wait_ge(gate_ps, 1)
            step(nc.vector.tensor_tensor(GL[:, :, :], ps[:, 3, 0:NT * NE].rearrange("p (t e) -> p t e", e=NE), GB[:, :].unsqueeze(1).broadcast_to([P, NT, NE]), ALU.add))
            step(nc.vector.tensor_reduce(GM[:, :], GL[:, :, :], AX.X, ALU.max))
            nc.vector.tensor_tensor(GL[:, :, :], GL[:, :, :], GM[:, :].unsqueeze(2).broadcast_to([P, NT, NE]), ALU.subtract).then_inc(gate_sub, 1)
            dve.wait_ge(gate_exp, 1)
            step(nc.vector.tensor_reduce(GM[:, :], GL[:, :, :], AX.X, ALU.add))
            step(nc.vector.reciprocal(GM[:, :], GM[:, :]))
            step(nc.vector.tensor_tensor(GL[:, :, :], GL[:, :, :], GM[:, :].unsqueeze(2).broadcast_to([P, NT, NE]), ALU.mult))
            step(nc.vector.memset(RANK[:, :, :], 0.0))
            for a in range(NE):
                for b in range(a + 1, NE):
                    step(nc.vector.tensor_tensor(GX[:, :], GL[:, :, b], GL[:, :, a], ALU.is_gt))
                    nc.vector.tensor_tensor(RANK[:, :, a], RANK[:, :, a], GX[:, :], ALU.add)
                    step(nc.vector.tensor_tensor(RANK[:, :, b], RANK[:, :, b], GX[:, :], ALU.subtract))
                    step(nc.vector.tensor_scalar(RANK[:, :, b], RANK[:, :, b], 1.0, None, ALU.add))
            step(nc.vector.tensor_scalar(RANK[:, :, :], RANK[:, :, :], 1.5, None, ALU.is_lt))
            nc.vector.tensor_tensor(keep["gates"][:, :].rearrange("p (e t) -> p t e", e=NE), GL[:, :, :], RANK[:, :, :], ALU.mult).then_inc(gates_ready, 1)
            done = dve.alloc_register("oh_blocks")
            dve.reg_mov(done, 0)
            with dve.Fori(0, NT) as w:
                lo = dve.value_load(blocks[0:1, 0, bass.ds(w, 1)], min_val=0, max_val=NB - 1)
                hi = dve.value_load(blocks[0:1, 1, bass.ds(w, 1)], min_val=1, max_val=NB)
                with dve.Fori(lo, hi) as b:
                    at = dve.snap(done, min_val=0, max_val=NT * NB)
                    for j in range(BLK):
                        dve.wait_ge(oh_free, at * BLK + j + 1)
                        nc.vector.tensor_scalar(ohs[0:EP, j, :], iota16[0:EP, :], keep["srcF"][:, bass.ds(b * BLK + j, 1)], None, ALU.is_equal)
                        nc.vector.tensor_scalar(ohd[0:EP, j, :], iota16[0:EP, bass.ds(w * P, P)], keep["dstF"][:, bass.ds(b * BLK + j, 1)], None, ALU.is_equal).then_inc(oh_ready, 1)
                    dve.reg_add(done, done, 1)
            dve.wait_ge(window_read, NT + 1)
            step(nc.vector.tensor_reduce(maxdeg[:, :], degf, AX.X, ALU.max))
            nc.vector.tensor_scalar(large[:, :], maxdeg[:, :], EXACT, None, ALU.is_gt).then_inc(large_ready, 1)
            step(nc.vector.tensor_scalar(INV[:, :], degf, 1.0, None, ALU.max))
            step(nc.vector.reciprocal(INV[:, :], INV[:, :]))
            step(nc.vector.tensor_scalar(degf, degf, 1.0, None, ALU.min))
            step(nc.vector.tensor_tensor(INV[:, :], INV[:, :], degf, ALU.mult))
            n = 0
            for t0, nt in SPANS:
                for k in range(KT):
                    dve.wait_ge(agg_ps, n + 1)
                    nc.vector.tensor_tensor(AGX[:, k, t0 * P:(t0 + nt) * P], ps[:, 4 + n % 4, 0:nt * P], INV[:, t0 * P:(t0 + nt) * P], ALU.mult).then_inc(agg_read, 1)
                    n += 1
            dve.sem_inc(dense_read, 2)
            dve.sem_inc(relu_done, 2)
            with dve.Fori(0, NE) as e:
                def biased(l, t):
                    dve.wait_ge(dense_ps, e * (2 * NT) + l * NT + t + 1)
                    if t == 0:
                        dve.wait_ge(bias_loaded, e * 32 + 16 * (l + 1))
                    dve.wait_ge(relu_done, e * (2 * NT) + l * NT + t + 1)
                    nc.vector.tensor_tensor(T1[:, t % 2, :], ps[:, t % 2, :], BB[:, l, :], ALU.add).then_inc(dense_read, 1)

                def low(t):
                    dve.wait_ge(relu_done, e * (2 * NT) + t + 3)
                    nc.vector.scalar_tensor_tensor(HL[:, t, :], T1[:, t % 2, :], 0.0, HH[:, t, :].bitcast(F32), ALU.max, ALU.subtract).then_inc(low_ready, 1)
                    dve.wait_ge(low_ready, e * NT + t + 2)

                for t in range(NT):
                    biased(0, t)
                    if t >= 1:
                        low(t - 1)
                low(NT - 1)
                n = 0
                for t0, nt in SPANS:
                    for k in range(KT):
                        dve.wait_ge(agg_ps, (e + 1) * (len(SPANS) * KT) + n + 1)
                        nc.vector.tensor_tensor(AG1[:, k, 0:nt * P], ps[:, 4 + n % 4, 0:nt * P], INV[:, t0 * P:(t0 + nt) * P], ALU.mult).then_inc(agg_read, 1)
                        n += 1
                    for t in range(t0, t0 + nt):
                        biased(1, t)
            dve.wait_ge(y_added, NE * NT + 2)
            normalize(nc, step, X, STATS, MV, RSTD, std_ready, var_ready, 1, 1, dve, MID).then_inc(mid_ready, 1)

        @block.tensor
        def _(pe):
            pe.wait_ge(consts, 1)
            pe.wait_ge(ind_ready, 1)
            for b in range(4):
                mm = nc.tensor.matmul(ps[0:1, 4 + b, 0:400], ones16[0:EP, 0:1], ind.rearrange("p w k -> p (w k)")[:, b * 400:(b + 1) * 400], start=True, stop=True)
            mm.then_inc(counts_ps, 1)
            pe.wait_ge(x_loaded, 32)
            n = 0
            for t0, nt in SPANS:
                for k in range(KT):
                    if n >= 2:
                        pe.wait_ge(tr_read, n - 1)
                    for t in range(nt):
                        mm = nc.tensor.transpose(ps[:, 2 + n % 2, t * P:(t + 1) * P], X[:, t0 + t, k * P:(k + 1) * P], ident[:, :])
                    mm.then_inc(tr_ps, 1)
                    n += 1
            pe.wait_ge(tr_read, n)
            pe.wait_ge(gate_loaded, 48)
            for t in range(NT):
                for k in range(KT):
                    mm = nc.tensor.matmul(ps[:, 3, t * NE:(t + 1) * NE], XT[:, k, t * P:(t + 1) * P], GW[:, k, :], start=(k == 0), stop=(k == KT - 1))
            mm.then_inc(gate_ps, 1)
            pe.wait_ge(ranges_ready, 1)
            pe.sem_inc(oh_free, BLK)
            done = pe.alloc_register("oh_blocks_pe")
            pe.reg_mov(done, 0)
            with pe.Fori(0, NT) as w:
                lo = pe.value_load(blocks[0:1, 0, bass.ds(w, 1)], min_val=0, max_val=NB - 1)
                hi = pe.value_load(blocks[0:1, 1, bass.ds(w, 1)], min_val=1, max_val=NB)
                pe.wait_ge(window_read, w + 1)
                for b, width in enumerate((4 * P, 4 * P, 3 * P)):
                    nc.tensor.matmul(ps[:, b, 0:width], zero16[:, :], iota16[:, 0:width].bitcast(BF16), start=True, stop=False)
                with pe.Fori(lo, hi) as blk:
                    at = pe.snap(done, min_val=0, max_val=NT * NB)
                    for j in range(BLK):
                        pe.wait_ge(oh_ready, at * BLK + j + 1)
                        for s in range(NT):
                            nc.tensor.matmul(ps[:, s // 4, (s % 4) * P:(s % 4 + 1) * P], ohs[0:EP, j, s * P:(s + 1) * P], ohd[0:EP, j, :], start=False, stop=False, skip_group_check=True)
                        nc.tensor.matmul(ps[:, 2, 2 * P:3 * P], ones16[0:EP, :], ohd[0:EP, j, :], start=False, stop=False, skip_group_check=True).then_inc(oh_free, 1)
                    pe.reg_add(done, done, 1)
                for b, width in enumerate((4 * P, 4 * P, 3 * P)):
                    mm = nc.tensor.matmul(ps[:, b, 0:width], zero16[:, :], iota16[:, 0:width].bitcast(BF16), start=False, stop=True)
                mm.then_inc(window_ps, 1)
            pe.wait_ge(window_read, NT + 1)

            pe.wait_ge(large_ready, 1)
            beyond = pe.value_load(large[0:1, 0:1], min_val=0, max_val=1)

            def sum_rows(k, bank, t0, nt, counts, dt):
                for s in range(NT):
                    for part in (HH, HL):
                        mm = nc.tensor.matmul(ps[:, bank, 0:nt * P], part[:, s, k * P:(k + 1) * P].bitcast(dt), counts[:, s, t0 * P:(t0 + nt) * P], start=(s == 0 and part is HH), stop=(s == NT - 1 and part is HL))
                mm.then_inc(agg_ps, 1)

            def aggregate(t0, nt, n, before):
                for k in range(KT):
                    before(n + k)
                    with pe.If(beyond < 1):
                        sum_rows(k, 4 + (n + k) % 4, t0, nt, ATR, F32R)
                    with pe.If(beyond > 0):
                        sum_rows(k, 4 + (n + k) % 4, t0, nt, AT, F32)

            pe.wait_ge(low_ready, 1)
            n = 0
            for t0, nt in SPANS:
                aggregate(t0, nt, n, lambda m: pe.wait_ge(agg_read, m - 3) if m >= 4 else None)
                n += KT
            pe.wait_ge(agg_read, n)
            with pe.Fori(0, NE) as e:
                def transposed(t):
                    pe.wait_ge(tr_read, e * NT + len(SPANS) * KT + t - 1)
                    for k in range(KT):
                        for part in (HH, HL):
                            mm = nc.tensor.matmul(ps[:, 2 + t % 2, k * P:(k + 1) * P], part[:, t, k * P:(k + 1) * P], identr[:, :], start=(part is HH), stop=(part is HL))
                    mm.then_inc(tr_ps, 1)

                def dense(l, t, agg, own, a, o):
                    if t == 0:
                        pe.wait_ge(weights_loaded, e * 64 + 32 * (l + 1))
                    pe.wait_ge(dense_read, e * (2 * NT) + l * NT + t + 1)
                    for k in range(KT):
                        nc.tensor.matmul(ps[:, t % 2, :], agg[:, k, a * P:(a + 1) * P], WL[:, k, :], start=(k == 0), stop=False)
                    for k in range(KT):
                        mm = nc.tensor.matmul(ps[:, t % 2, :], own[:, k, o * P:(o + 1) * P], WR[:, k, :], start=False, stop=(k == KT - 1))
                    mm.then_inc(dense_ps, 1)

                for t in range(NT):
                    dense(0, t, AGX, XT, t, t)
                pe.wait_ge(low_ready, (e + 1) * NT + 1)
                n = 0
                for t0, nt in SPANS:
                    aggregate(t0, nt, n, lambda m: pe.wait_ge(agg_read, (e + 1) * (len(SPANS) * KT) + m - 3))
                    n += KT
                    for t in range(t0, t0 + nt):
                        transposed(t)
                    pe.wait_ge(agg_read, (e + 1) * (len(SPANS) * KT) + n)
                    pe.wait_ge(tr_read, e * NT + len(SPANS) * KT + t0 + nt)
                    for t in range(t0, t0 + nt):
                        dense(1, t, AG1, H1T, t - t0, t - t0)


def messages_block(nc, top, dram, keep):
    ctx = ExitStack()
    with ctx:
        def sb(name, shape, dt=F32):
            return ctx.enter_context(nc.sbuf_tensor(name, shape, dt))

        def sem(name):
            return ctx.enter_context(nc.semaphore(name))

        SUM = sb("SUM", [P, NT, PATHS * EXT])
        X1 = sb("X1", [P, 2, G, D])
        X2 = sb("X2", [P, 2, G, D])
        PR = sb("PR", [P, 2, G, CW])
        DIF = sb("DIF", [P, 2, G, P], FP16)
        SQ = sb("SQ", [P, G, P])
        S = sb("S", [P, 2, G, P])
        IDX = sb("IDX", [P, 2, G], I32)
        iota_i = sb("iota_i", [P, P], I32)
        iota_f = sb("iota_f", [P, P])
        wbase = sb("wbase", [P, NT])
        zero16 = sb("zero16b", [P, P], BF16)
        zrow16 = sb("zrow16b", [P, CW], BF16)
        STATS = sb("STATSb", [P, NT, 6])
        MV = sb("MVb", [P, NT, 2])
        RSTD = sb("RSTDb", [P, NT])
        ROW = X1[:, :, :, :].rearrange("p a g d -> p (a g) d")[:, 0:NT, :]
        OUT = PR[:, :, :, :].rearrange("p a g d -> p (a g) d")[:, 0:NT, :]
        ps = ctx.enter_context(nc.psum_tensor("psb", [P, 8, D], F32))

        x2_loaded = [sem(f"x2_loaded{i}") for i in range(2)]
        x1_loaded = [sem(f"x1_loaded{i}") for i in range(2)]
        idx_ready, waited, waited_v, sum_zeroed = sem("idx_ready"), sem("waited"), sem("waited_v"), sem("sum_zeroed")
        consts, iota_sem, zeroed = sem("constsb"), sem("iota_semb"), sem("zeroed")
        dif_ready, dif_used = sem("dif_ready"), sem("dif_used")
        products_ready = sem("products_ready")
        sq_done = sem("sq_done")
        onehot_ready, sums_ps, sums_read = sem("onehot_ready"), sem("sums_ps"), sem("sums_read")
        res_loaded, var_ready, std_ready, out_ready, out_stored = sem("res_loaded"), sem("var_readyb"), sem("std_readyb"), sem("out_ready"), sem("out_stored")
        chain_v = sem("chain_vb")
        block = ctx.enter_context(nc.Block())

        def windows_of(eng, regs, g):
            eng.load(regs, keep["windows"][0:1, bass.ds(g, 1), :].rearrange("p a k -> p (a k)"))

        def bounds(eng, regs):
            return eng.snap(regs[0], min_val=0, max_val=NT - 1), eng.snap(regs[1], min_val=1, max_val=NT)

        def groups(eng, body):
            with eng.Fori(0, NG // 2) as turn:
                for half in range(2):
                    body(turn * 2 + half, half, turn)

        @block.sync
        def _(sp):
            def load(g, half, turn):
                sp.wait_ge(products_ready, (g + 1) * NC)
                sp.dma_start(X2[0:EP, half, :, :], dram["edge_attr"][bass.ds(g * (G * EP), G * EP), :].rearrange("(g p) d -> p g d", p=EP)).then_inc(x2_loaded[half], 16)
            groups(sp, load)
            sp.wait_ge(products_ready, (NG + 2) * NC)
            sp.dma_start(ROW, dram["x_mid"].rearrange("(t p) d -> p t d", p=P)).then_inc(res_loaded, 16)
            sp.wait_ge(out_ready, 1)
            sp.dma_start(dram["out"][0:(NT - 1) * P, :].rearrange("(t p) d -> p t d", p=P), OUT[:, 0:NT - 1, :]).then_inc(out_stored, 16)
            sp.dma_start(dram["out"][(NT - 1) * P:N, :], OUT[0:LAST, NT - 1, :]).then_inc(out_stored, 16)
            sp.wait_ge(out_stored, 32)

        @block.gpsimd
        def _(pool):
            nc.gpsimd.iota(iota_i[:, :], [[1, P]], base=0, channel_multiplier=0).then_inc(iota_sem, 1)
            pool.wait_ge(iota_sem, 1)
            nc.gpsimd.tensor_copy(iota_f[:, :], iota_i[:, :]).then_inc(consts, 1)
            pool.wait_ge(consts, 1)

            def gather(g, half, turn):
                pool.wait_ge(products_ready, (g + 1) * NC)
                dst = keep["dstF"][:, bass.ds(g * G, G)]
                pool.wait_ge(dif_used, g + 1)
                nc.gpsimd.tensor_tensor(DIF[0:EP, half, :, :], iota_f[0:EP, :].unsqueeze(1).broadcast_to([EP, G, P]), dst.unsqueeze(2).broadcast_to([EP, G, P]), ALU.subtract).then_inc(dif_ready, 1)
                nc.gpsimd.tensor_copy(IDX[0:EP, half, :], keep["src"][:, bass.ds(g * G, G)]).then_inc(idx_ready, 1)
                pool.wait_ge(idx_ready, g + 1)
                pool.sem_inc(waited, 1)
                for j in range(G):
                    nc.gpsimd.indirect_dma_start(out=X1[0:EP, half, j, :], out_offset=None, in_=dram["x_mid"],
                                                 in_offset=bass.IndirectOffsetOnAxis(ap=IDX[0:EP, half, j:j + 1], axis=0)).then_inc(x1_loaded[half], 16)
            for half in range(2):
                gather(half, half, 0)
            nc.gpsimd.memset(SUM[:, ZV:NT, :], 0.0).then_inc(sum_zeroed, 1)
            with pool.Fori(1, NG // 2) as turn:
                for half in range(2):
                    gather(turn * 2 + half, half, turn)

        @block.vector
        def _(dve):
            step = Chain(dve, chain_v)
            for w in range(NT):
                nc.vector.memset(wbase[:, w:w + 1], float(w * P))
            nc.vector.memset(zero16[:, :], 0.0)
            step(nc.vector.memset(zrow16[:, :], 0.0))
            nc.vector.memset(SUM[:, 0:ZV, :], 0.0).then_inc(sum_zeroed, 1)
            for credit in (dif_used, sums_ps, sums_read):
                dve.sem_inc(credit, 2)
            dve.sem_inc(products_ready, 2 * NC)
            dve.sem_inc(zeroed, 1)
            dve.wait_ge(consts, 1)
            pairs = dve.alloc_register("pairs_v")
            span = [dve.alloc_register(f"span_v{i}") for i in range(2)]
            ahead = [dve.alloc_register(f"ahead_v{i}") for i in range(2)]
            windows_of(dve, span, 0)
            dve.reg_mov(pairs, 0)

            def next_windows():
                for r, q in zip(span, ahead):
                    dve.reg_mov(r, q)

            def add_sums(c):
                lo, hi = bounds(dve, span)
                with dve.Fori(lo, hi) as w:
                    at = dve.snap(pairs, min_val=0, max_val=NT * NG * NC)
                    dve.wait_ge(sums_ps, at + 3)
                    acc = SUM[:, bass.ds(w, 1), c * CW:(c + 1) * CW]
                    nc.vector.tensor_tensor(acc, acc, ps[:, bass.ds((w % 2) * NC + c, 1), :], ALU.add).then_inc(sums_read, 1)
                    dve.reg_add(pairs, pairs, 1)

            def load_paths(c):
                regs = [dve.alloc_register(f"path_off{next(made)}") for _ in range(2 * PC)]
                dve.load(regs[0:PC], keep["path"][0:1, c * PC:(c + 1) * PC])
                dve.load(regs[PC:], keep["path"][0:1, PATHS + c * PC:PATHS + (c + 1) * PC])
                return [dve.snap(r, True, min_val=0, max_val=D - EXT) for r in regs]

            paths, made = [None], count()

            def products(g, half, turn):
                if half == 0:
                    paths[0] = load_paths(0)
                for c in range(NC):
                    off = paths[0]
                    if c == 0:
                        dve.wait_ge(x1_loaded[half], turn * (16 * G) + 16 * G)
                        dve.wait_ge(x2_loaded[half], turn * 16 + 16)
                    for j in range(PC):
                        ins = nc.vector.tensor_tensor(PR[0:EP, c % 2, :, j * EXT:(j + 1) * EXT], X1[0:EP, half, :, bass.ds(off[j], EXT)], X2[0:EP, half, :, bass.ds(off[PC + j], EXT)], ALU.mult)
                    ins.then_inc(products_ready, 1)
                    if (half, c) != (1, NC - 1):
                        paths[0] = load_paths((c + 1) % NC)
                    if c >= 1:
                        add_sums(c - 1)
                    elif half:
                        windows_of(dve, ahead, g)
                        add_sums(NC - 1)
                        next_windows()
                    else:
                        windows_of(dve, ahead, g)
                        with dve.If(turn > 0):
                            add_sums(NC - 1)
                        with dve.If(turn < 1):
                            dve.wait_ge(sum_zeroed, 2)
                            dve.sem_inc(waited_v, 1)
                        next_windows()

            groups(dve, products)
            add_sums(NC - 1)
            dve.wait_ge(res_loaded, 16)
            for c in range(PATHS // (2 * PC)):
                regs = [dve.alloc_register(f"seg_off{c}_{i}") for i in range(2 * PC)]
                dve.load(regs, keep["path"][0:1, 2 * PATHS + c * 2 * PC:2 * PATHS + (c + 1) * 2 * PC])
                off = [dve.snap(r, True, min_val=0, max_val=D - EXT) for r in regs]
                for j in range(2 * PC):
                    p = c * 2 * PC + j
                    seg = ROW[:, :, bass.ds(off[j], EXT)]
                    step(nc.vector.scalar_tensor_tensor(seg, SUM[:, :, p * EXT:(p + 1) * EXT], keep["coef"][:, p:p + 1], seg, ALU.mult, ALU.add))
            normalize(nc, step, ROW, STATS, MV, RSTD, std_ready, var_ready, 1, 1, dve, OUT).then_inc(out_ready, 1)

        @block.scalar
        def _(act):
            made = act.alloc_register("pairs_a")
            span = [act.alloc_register(f"span_a{i}") for i in range(2)]
            act.reg_mov(made, 0)
            act.sem_inc(onehot_ready, 1)
            act.wait_ge(zeroed, 1)

            def onehots(g, half, turn):
                act.wait_ge(dif_ready, g + 1)
                windows_of(act, span, g)
                lo, hi = bounds(act, span)
                for c in range(NC):
                    with act.Fori(lo, hi) as w:
                        at = act.snap(made, min_val=0, max_val=NT * NG * NC)
                        act.wait_ge(onehot_ready, at + 1)
                        nc.scalar.activation(SQ[0:EP, :, :], DIF[0:EP, half, :, :], ACT.Square, bias=wbase[0:EP, bass.ds(w, 1)]).then_inc(sq_done, 1)
                        act.wait_ge(sq_done, at + 1)
                        act.wait_ge(sums_ps, at + 1)
                        nc.scalar.activation(S[0:EP, bass.ds(at % 2, 1), :, :].rearrange("p a g n -> p (a g) n"), SQ[0:EP, :, :], ACT.Relu, bias=1.0, scale=-1.0).then_inc(onehot_ready, 1)
                        act.reg_add(made, made, 1)
                act.drain().then_inc(dif_used, 1)
            groups(act, onehots)
            act.wait_ge(var_ready, 1)
            nc.scalar.activation(RSTD[:, :], RSTD[:, :], ACT.Sqrt).then_inc(std_ready, 1)

        @block.tensor
        def _(pe):
            pe.wait_ge(zeroed, 1)
            pairs = pe.alloc_register("pairs_t")
            span = [pe.alloc_register(f"span_t{i}") for i in range(2)]
            flags = [pe.alloc_register(f"here{j}") for j in range(G)]
            pe.reg_mov(pairs, 0)

            def sums(g, half, turn):
                windows_of(pe, span, g)
                lo, hi = bounds(pe, span)
                for c in range(NC):
                    with pe.Fori(lo, hi) as w:
                        pe.wait_ge(products_ready, (g + 2) * NC + c + 1)
                        at = pe.snap(pairs, min_val=0, max_val=NT * NG * NC)
                        pe.wait_ge(onehot_ready, at + 2)
                        pe.wait_ge(sums_read, at + 1)
                        bank = ps[:, bass.ds((w % 2) * NC + c, 1), :].rearrange("p a n -> p (a n)")
                        pe.load(flags, keep["present"][0:1, bass.ds(w, 1), bass.ds(g * G, G)].rearrange("p a k -> p (a k)"))
                        here = [pe.snap(r, min_val=0, max_val=1) for r in flags]
                        nc.tensor.matmul(bank, zero16[0:EP, :], zrow16[0:EP, :], start=True, stop=True)
                        for slot in range(2):
                            with pe.If(at % 2 < 1 if slot == 0 else at % 2 > 0):
                                for j in range(G):
                                    with pe.If(here[j] > 0):
                                        nc.tensor.matmul(bank, S[0:EP, slot, j, :], PR[0:EP, c % 2, j, :], start=False, stop=True, skip_group_check=True)
                        nc.tensor.matmul(bank[:, 0:1], zero16[0:EP, :], zrow16[0:EP, 0:1], start=False, stop=True, skip_group_check=True).then_inc(sums_ps, 1)
                        pe.reg_add(pairs, pairs, 1)
            groups(pe, sums)


def gnn_kernel(nc, x, srcT, dstT, edge_attr, gate_W, gate_b, Wl, bl, Wr, coeffs, paths, out):
    ctx = ExitStack()
    with ctx:
        x_mid = nc.dram_tensor("x_mid", (NP, D), F32, kind="Internal").ap()
        dram = dict(x=x, srcT=srcT, dstT=dstT, edge_attr=edge_attr, gate_W=gate_W, gate_b=gate_b,
                    Wl=Wl, bl=bl, Wr=Wr, coeffs=coeffs, paths=paths, out=out, x_mid=x_mid)
        keep = {}
        for name, shape, dt in (("src", [EP, ET], I32), ("dst", [EP, ET], I32), ("srcF", [EP, ET], F32),
                                ("dstF", [EP, ET], F32), ("path", [1, 3 * PATHS], I32), ("coef", [P, PATHS], F32),
                                ("gates", [P, NE * NT], F32), ("present", [1, NT, ET], mybir.dt.uint8),
                                ("windows", [1, NG, 2], I32)):
            keep[name] = ctx.enter_context(nc.sbuf_tensor(name + "_kept", shape, dt))
        experts_block(nc, ctx, dram, keep)
        messages_block(nc, ctx, dram, keep)


def kernel(x, src, dst, edge_attr_512, L0_gnn_gate_W, L0_gnn_gate_b, L0_gnn_Wl, L0_gnn_bl, L0_gnn_Wr,
           L1_gnn_path_coeffs, L1_gnn_path_indices):
    import numpy as np
    import concourse.bacc as bacc
    from concourse.bass_utils import run_bass_kernel_spmd

    c = np.ascontiguousarray
    arrays = {
        "x": c(x),
        "srcT": c(np.asarray(src).reshape(ET, EP).T),
        "dstT": c(np.asarray(dst).reshape(ET, EP).T),
        "edge_attr": c(edge_attr_512),
        "gate_W": c(L0_gnn_gate_W), "gate_b": c(L0_gnn_gate_b),
        "Wl": c(L0_gnn_Wl), "bl": c(L0_gnn_bl), "Wr": c(L0_gnn_Wr),
        "coeffs": c(L1_gnn_path_coeffs),
        "paths": c(np.asarray(L1_gnn_path_indices).T).reshape(3 * PATHS),
    }
    nc = bacc.Bacc("TRN2", target_bir_lowering=False, num_devices=1)
    args = [nc.dram_tensor(f"in_{k}", a.shape, mybir.dt.from_np(a.dtype), kind="ExternalInput").ap() for k, a in arrays.items()]
    out = nc.dram_tensor("out_dram", (N, D), F32, kind="ExternalOutput").ap()
    gnn_kernel(nc, *args, out)
    r = run_bass_kernel_spmd(nc, [{f"in_{k}": a for k, a in arrays.items()}], core_ids=[0])
    return r.results[0]["out_dram"]
```

```python
import concourse.bass as bass
from concourse import mybir
from contextlib import ExitStack
from itertools import count

F32 = mybir.dt.float32
F32R = mybir.dt.float32r
BF16 = mybir.dt.bfloat16
FP16 = mybir.dt.float16
I32 = mybir.dt.int32
ALU = mybir.AluOpType
ACT = mybir.ActivationFunctionType
AX = mybir.AxisListType

P = 128
N = 1250
NT = (N + P - 1) // P
NP = NT * P
LAST = N - (NT - 1) * P
D = 512
KT = D // P
NE = 4
E = 20000
EP = 125
ET = E // EP
EXT, PATHS = 32, 64
BLK = 4
NB = ET // BLK
G = 8
NG = ET // G
SPLIT = 2
FIRST, OTHER = 2, 1
PC = 16
NC = PATHS // PC
CW = PC * EXT
SPANS = [(0, 4), (4, 4), (8, 2)]
EPS = 1e-5
EXACT = 2048.0
ZV, ZA = 4, 6


class Chain:

    def __init__(self, eng, sem):
        self.eng, self.sem, self.n = eng, sem, 0

    def __call__(self, ins, running=0):
        self.n += 1
        ins.then_inc(self.sem, 1)
        if self.n > running:
            self.eng.wait_ge(self.sem, self.n - running)


def normalize(nc, dve, step, rows, out, t0, nt, scratch, var_ready, std_ready, turn, ready):
    stats, mv, rstd = scratch
    here = rstd[:, t0:t0 + nt]
    for t in range(t0, t0 + nt):
        nc.vector.bn_stats(stats[:, t, :], rows[:, t, :])
    step(nc.vector.memset(here, 0.0))
    for t in range(t0, t0 + nt):
        nc.vector.bn_aggr(mv[:, t, :], stats[:, t, :])
    step(nc.vector.memset(here, 0.0))
    nc.vector.tensor_scalar(here, mv[:, t0:t0 + nt, 1], EPS, None, ALU.add).then_inc(var_ready, 1)
    dve.wait_ge(std_ready, turn + 1)
    step(nc.vector.reciprocal(here, here))
    for t in range(t0, t0 + nt):
        ins = nc.vector.tensor_scalar(out[:, t, :], rows[:, t, :], mv[:, t, 0:1], rstd[:, t:t + 1],
                                      ALU.subtract, ALU.mult)
        if t + 1 in [s0 + n for s0, n in SPANS]:
            ins.then_inc(ready, 1)


def experts_block(nc, dram, keep):
    ctx = ExitStack()
    with ctx:
        def sb(name, shape, dt=F32):
            return ctx.enter_context(nc.sbuf_tensor(name, shape, dt))

        def sem(name):
            return ctx.enter_context(nc.semaphore(name))

        dst = sb("dst", [EP, ET], I32)
        srcF = sb("srcF", [EP, ET])
        X = sb("X", [P, NT, D])
        XT = sb("XT", [P, KT, NP])
        AT = sb("AT", [P, NT, NP])
        ATR = AT[:, :, :].bitcast(F32R)
        AGX = keep["shared"][:, :].rearrange("p (k n) -> p k n", k=KT)
        HH = sb("HH", [P, NT, D], F32R)
        HL = sb("HL", [P, NT, D], F32R)
        H1T = sb("H1T", [P, KT, 4 * P])
        AG1 = sb("AG1", [P, KT, 4 * P])
        W = sb("W", [P, 2, KT, D])
        WL, WR = W[:, 0, :, :], W[:, 1, :, :]
        BB = sb("BB", [P, 2, D])
        INV = sb("INV", [P, NP])
        BIASED = sb("BIASED", [P, 2, D])
        GATED = sb("GATED", [P, 2, D])
        GW = sb("GW", [P, KT, NE])
        GB = sb("GB", [P, NE])
        GL = sb("GL", [P, NT, NE])
        RANK = sb("RANK", [P, NT, NE])
        GM = sb("GM", [P, NT])
        GX = sb("GX", [P, NT])
        STATS = sb("STATS", [P, NT, 6])
        MV = sb("MV", [P, NT, 2])
        RSTD = sb("RSTD", [P, NT])
        wbytes = W[:, :, :, :].rearrange("p a k d -> p (a k d)")
        ohs = wbytes.bitcast(BF16)[:, NP:NP + BLK * NP].rearrange("p (b n) -> p b n", b=BLK)
        ohd = H1T[:, :, :].rearrange("p t d -> p (t d)").bitcast(BF16)[:, 0:BLK * P].rearrange("p (b n) -> p b n", b=BLK)
        iota16 = wbytes.bitcast(FP16)[:, 0:NP]
        iota32 = AGX[:, 0, :].bitcast(I32)
        ge = AGX[:, 1:3, :].rearrange("p t d -> p (t d)").bitcast(BF16)[0:EP, 0:(NT + 1) * ET].rearrange("p (w k) -> p w k", w=NT + 1)
        ind = AGX[:, 3, :].bitcast(BF16)[0:EP, 0:NT * ET].rearrange("p (w k) -> p w k", w=NT)
        ones16 = sb("ones16", [P, P], BF16)
        zero16 = sb("zero16", [P, P], BF16)
        ident = sb("ident", [P, P])
        identr = sb("identr", [P, P], F32R)
        maxdeg = sb("maxdeg", [P, 1])
        large = sb("large", [P, 1], I32)
        MID = XT[:, :, :].rearrange("p k n -> p (k n)").rearrange("p (t d) -> p t d", d=D)
        cnt = H1T[0:1, :, :].rearrange("p t d -> p (t d)")[:, BLK * P // 2:BLK * P // 2 + NT * ET].rearrange("p (w k) -> p w k", w=NT)
        scratch_row = AG1[0:1, :, :].rearrange("p t d -> p (t d)")
        degf = AG1[:, :, :].rearrange("p t d -> p (t d)")[:, 0:NP]
        blocks = sb("blocks", [1, 2, NT], I32)
        ps = ctx.enter_context(nc.psum_tensor("ps", [P, 8, D], F32))

        x_loaded = [sem(f"x_loaded{i}") for i in range(len(SPANS))]
        idx_loaded, gate_loaded = sem("idx_loaded"), sem("gate_loaded")
        left_loaded, right_loaded, bias_loaded = sem("left_loaded"), sem("right_loaded"), sem("bias_loaded")
        left_used = sem("left_used")
        x_zeroed, consts, iota_i = sem("x_zeroed"), sem("consts"), sem("iota_i")
        ind_ready, counts_ps = sem("ind_ready"), sem("counts_ps")
        counts_read = sem("counts_read")
        ranges_ready = sem("ranges_ready")
        oh_ready, oh_free = sem("oh_ready"), sem("oh_free")
        window_ps, degrees_read, window_read = sem("window_ps"), sem("degrees_read"), sem("window_read")
        tr_ps, tr_read = sem("tr_ps"), sem("tr_read")
        logits_read = sem("logits_read")
        gate_ps, gate_sub, gate_exp = sem("gate_ps"), sem("gate_sub"), sem("gate_exp")
        high_ready, low_ready, large_ready = sem("high_ready"), sem("low_ready"), sem("large_ready")
        agg_ps, agg_read = sem("agg_ps"), sem("agg_read")
        dense_ps, dense_read = sem("dense_ps"), sem("dense_read")
        relu_done, y_added = sem("relu_done"), sem("y_added")
        var_ready, std_ready, mid_ready, mid_stored = sem("var_ready"), sem("std_ready"), sem("mid_ready"), sem("mid_stored")
        chain_v, chain_p = sem("chain_v"), sem("chain_p")
        block = ctx.enter_context(nc.Block())

        @block.sync
        def _(sp):
            sp.dma_start(keep["src"][:, :], dram["srcT"]).then_inc(idx_loaded, 16)
            sp.dma_start(dst[:, :], dram["dstT"]).then_inc(idx_loaded, 16)
            sp.dma_start(keep["path"][:, :], dram["paths"].rearrange("(a n) -> a n", a=1)).then_inc(idx_loaded, 16)
            for (t0, nt), loaded in zip(SPANS, x_loaded):
                whole = min(nt, NT - 1 - t0)
                sp.dma_start(X[:, t0:t0 + whole, :], dram["x"][t0 * P:(t0 + whole) * P, :].rearrange("(t p) d -> p t d", p=P)).then_inc(loaded, 16)
            sp.wait_ge(x_zeroed, 1)
            sp.dma_start(X[0:LAST, NT - 1, :], dram["x"][(NT - 1) * P:N, :]).then_inc(x_loaded[-1], 16)
            sp.dma_start(GW[:, :, :], dram["gate_W"].rearrange("(k p) e -> p k e", p=P)).then_inc(gate_loaded, 16)
            sp.dma_start(GB[:, :], dram["gate_b"].partition_broadcast(P)).then_inc(gate_loaded, 16)
            sp.dma_start(keep["coef"][:, :], dram["coeffs"].partition_broadcast(P)).then_inc(gate_loaded, 16)
            with sp.Fori(0, NE) as e:
                for l in range(2):
                    sp.wait_ge(left_used, e * 2 + l + 1)
                    sp.dma_start(WL[:, :, :], dram["Wl"][bass.ds(e, 1), l, :, :].rearrange("e (k p) o -> p (e k) o", p=P)).then_inc(left_loaded, 16)
                    sp.wait_ge(dense_ps, e * (2 * NT) + l * NT + 1)
                    sp.dma_start(WR[:, :, :], dram["Wr"][bass.ds(e, 1), l, :, :].rearrange("e (k p) o -> p (e k) o", p=P)).then_inc(right_loaded, 16)
                    sp.dma_start(BB[:, l, :], dram["bl"][bass.ds(e, 1), l, :].rearrange("e d -> (e d)").partition_broadcast(P)).then_inc(bias_loaded, 16)
            sp.wait_ge(left_used, NE * 2)
            sp.dma_start(keep["x2"][0:EP, :, :], dram["edge_attr"][0:G * EP, :].rearrange("(g p) d -> p g d", p=EP)).then_inc(keep["x2_loaded"], 16)
            for i, (t0, nt) in enumerate(SPANS):
                sp.wait_ge(mid_ready, i + 1)
                sp.dma_start(dram["x_mid"][t0 * P:(t0 + nt) * P, :].rearrange("(t p) d -> p t d", p=P), MID[:, t0:t0 + nt, :]).then_inc(mid_stored, 16)
            sp.wait_ge(mid_stored, 16 * len(SPANS))

        @block.gpsimd
        def _(pool):
            step = Chain(pool, chain_p)
            nc.gpsimd.memset(X[:, NT - 1, :], 0.0).then_inc(x_zeroed, 1)
            nc.gpsimd.iota(iota32, [[1, NP]], base=0, channel_multiplier=0).then_inc(iota_i, 1)
            nc.gpsimd.memset(ones16[:, :], 1.0)
            nc.gpsimd.memset(zero16[:, :], 0.0)
            step(nc.gpsimd.memset(ident[:, :], 0.0))
            nc.gpsimd.affine_select(out=ident[:, :], in_=ident[:, :], compare_op=ALU.not_equal, fill=1.0,
                                    base=0, pattern=[[-1, P]], channel_multiplier=1).then_inc(consts, 1)
            pool.sem_inc(y_added, 2)
            with pool.Fori(0, NE) as e:
                for t in range(NT):
                    pool.wait_ge(relu_done, e * (2 * NT) + NT + t + 3)
                    nc.gpsimd.tensor_tensor(X[:, t, :], X[:, t, :], GATED[:, t % 2, :], ALU.add).then_inc(y_added, 1)

        @block.scalar
        def _(act):
            n = 0
            for t0, nt in SPANS:
                for k in range(KT):
                    act.wait_ge(tr_ps, n + 1)
                    nc.scalar.copy(XT[:, k, t0 * P:(t0 + nt) * P], ps[:, 2 + n % 2, 0:nt * P]).then_inc(tr_read, 1)
                    n += 1
            for t in range(NT):
                last = nc.scalar.copy(HH[:, t, :], X[:, t, :])
            last.then_inc(high_ready, 1)
            act.sem_inc(window_read, 2)
            with act.Fori(0, NT // 2) as turn:
                for half in range(2):
                    w = turn * 2 + half
                    act.wait_ge(window_ps, w + 1)
                    nc.scalar.copy(degf[:, bass.ds(w * P, P)], ps[:, half * 4 + 2, 2 * P:3 * P]).then_inc(degrees_read, 1)
                    for b, (t0, nt) in enumerate(SPANS):
                        last = nc.scalar.copy(AT[:, t0:t0 + nt, bass.ds(w * P, P)], ps[:, half * 4 + b, 0:nt * P].rearrange("p (t n) -> p t n", n=P))
                    last.then_inc(window_read, 1)
            act.wait_ge(gate_sub, 1)
            nc.scalar.activation(GL[:, :, :], GL[:, :, :], ACT.Exp).then_inc(gate_exp, 1)

            def root(i):
                t0, nt = SPANS[i]
                act.wait_ge(var_ready, i + 1)
                nc.scalar.activation(RSTD[:, t0:t0 + nt], RSTD[:, t0:t0 + nt], ACT.Sqrt).then_inc(std_ready, 1)

            with act.Fori(0, NE) as e:
                def gated(t):
                    act.wait_ge(dense_read, e * (2 * NT) + NT + t + 3)
                    act.wait_ge(y_added, e * NT + t + 1)
                    nc.scalar.activation(GATED[:, t % 2, :], BIASED[:, t % 2, :], ACT.Relu, scale=keep["gates"][:, bass.ds(e * NT + t, 1)]).then_inc(relu_done, 1)

                for t in range(NT):
                    act.wait_ge(dense_read, e * (2 * NT) + t + 3)
                    nc.scalar.activation(HH[:, t, :], BIASED[:, t % 2, :], ACT.Relu).then_inc(relu_done, 1)
                for t0, nt in SPANS:
                    for t in range(t0, t0 + nt):
                        act.wait_ge(tr_ps, e * NT + len(SPANS) * KT + t + 1)
                        nc.scalar.copy(H1T[:, :, (t - t0) * P:(t - t0 + 1) * P], ps[:, 2 + t % 2, :].rearrange("p (k n) -> p k n", n=P)).then_inc(tr_read, 1)
                    if t0 > 0:
                        with act.If(e > NE - 2):
                            root(SPANS.index((t0, nt)) - 1)
                    for t in range(t0, t0 + nt):
                        gated(t)
            root(len(SPANS) - 1)

        @block.vector
        def _(dve):
            step = Chain(dve, chain_v)
            dve.wait_ge(idx_loaded, 48)
            nc.vector.tensor_copy(srcF[:, :], keep["src"][:, :])
            nc.vector.tensor_scalar(keep["path"][:, :], keep["path"][:, :], EXT, None, ALU.mult)
            step(nc.vector.tensor_scalar(keep["dstF"][:, :], dst[:, :], -1.0, float(NP), ALU.max, ALU.min))
            for w in range(NT + 1):
                last = nc.vector.tensor_scalar(ge[:, w, :], keep["dstF"][:, :], float(w * P), None, ALU.is_ge)
            step(last)
            nc.vector.tensor_tensor(ind, ge[:, 0:NT, :], ge[:, 1:NT + 1, :], ALU.subtract).then_inc(ind_ready, 1)
            dve.wait_ge(iota_i, 1)
            dve.wait_ge(consts, 1)
            nc.vector.tensor_copy(identr[:, :], ident[:, :])
            step(nc.vector.tensor_copy(iota16, iota32))
            dve.wait_ge(counts_ps, 1)
            step(nc.vector.tensor_scalar(cnt.rearrange("p w k -> p (w k)").rearrange("p (b n) -> p b n", b=4), ps[0:1, 4:8, 0:400], 1.0, None, ALU.min))
            dve.sem_inc(counts_read, 1)
            step(nc.vector.tensor_copy(keep["present"][:, :, :], cnt))
            asc, bp, gp = scratch_row[:, 0:64], scratch_row[:, 64:64 + NT * NB], scratch_row[:, 500:500 + NT * NG]
            s3, m1 = scratch_row[:, 720:720 + NT * NB], scratch_row[:, 1130:1150]
            iotas, m2 = scratch_row[:, 1160:1210], scratch_row[:, 1220:1240]
            bp3, gp3 = bp.rearrange("p (w k) -> p w k", w=NT), gp.rearrange("p (w g) -> p w g", w=NT)
            step(nc.vector.tensor_copy(asc, iota32[0:1, 0:64]))
            nc.vector.tensor_reduce(bp3, cnt.rearrange("p w (b k) -> p w b k", k=BLK), AX.X, ALU.max)
            step(nc.vector.tensor_reduce(gp3, cnt.rearrange("p w (g k) -> p w g k", k=G), AX.X, ALU.max))

            def first_and_end(flags, size, n, lo, hi):
                s = s3[:, 0:n * size].rearrange("p (n s) -> p n s", n=n)
                r, q = m1[:, 0:n], iotas
                step(nc.vector.tensor_scalar(q[:, 0:size], asc[:, 0:size], -1.0, 100.0, ALU.mult, ALU.add))
                step(nc.vector.tensor_tensor(s, flags, q[:, 0:size].unsqueeze(1).broadcast_to([1, n, size]), ALU.mult))
                step(nc.vector.tensor_reduce(r, s, AX.X, ALU.max))
                step(nc.vector.tensor_scalar(r, r, -1.0, 100.0, ALU.mult, ALU.add))
                step(nc.vector.tensor_scalar(r, r, float(size - 1), None, ALU.min))
                step(nc.vector.tensor_copy(lo, r))
                step(nc.vector.tensor_scalar(r, r, 1.0, None, ALU.add))
                step(nc.vector.tensor_scalar(q[:, 0:size], asc[:, 0:size], 1.0, None, ALU.add))
                step(nc.vector.tensor_tensor(s, flags, q[:, 0:size].unsqueeze(1).broadcast_to([1, n, size]), ALU.mult))
                step(nc.vector.tensor_reduce(m2[:, 0:n], s, AX.X, ALU.max))
                step(nc.vector.tensor_tensor(r, r, m2[:, 0:n], ALU.max))
                step(nc.vector.tensor_copy(hi, r))

            first_and_end(bp3, NB, NT, blocks[:, 0, :], blocks[:, 1, :])
            first_and_end(gp3.rearrange("p w g -> p g w"), NT, NG, keep["windows"][:, :, 0], keep["windows"][:, :, 1])
            nc.vector.memset(m2, 0.0).then_inc(ranges_ready, 1)

            for i in range(len(SPANS)):
                dve.wait_ge(x_loaded[i], 32 if i == len(SPANS) - 1 else 16)
            dve.wait_ge(high_ready, 1)
            nc.vector.tensor_tensor(HL[:, :, :], X[:, :, :], HH[:, :, :].bitcast(F32), ALU.subtract).then_inc(low_ready, 1)

            def logits():
                dve.wait_ge(gate_loaded, 48)
                dve.wait_ge(gate_ps, 1)
                step(nc.vector.tensor_tensor(GL[:, :, :], ps[:, 7, 0:NT * NE].rearrange("p (t e) -> p t e", e=NE), GB[:, :].unsqueeze(1).broadcast_to([P, NT, NE]), ALU.add))
                dve.sem_inc(logits_read, 1)

            def gates():
                step(nc.vector.tensor_reduce(GM[:, :], GL[:, :, :], AX.X, ALU.max))
                nc.vector.tensor_tensor(GL[:, :, :], GL[:, :, :], GM[:, :].unsqueeze(2).broadcast_to([P, NT, NE]), ALU.subtract).then_inc(gate_sub, 1)
                dve.wait_ge(gate_exp, 1)
                step(nc.vector.tensor_reduce(GM[:, :], GL[:, :, :], AX.X, ALU.add))
                step(nc.vector.reciprocal(GM[:, :], GM[:, :]))
                step(nc.vector.tensor_tensor(GL[:, :, :], GL[:, :, :], GM[:, :].unsqueeze(2).broadcast_to([P, NT, NE]), ALU.mult))
                step(nc.vector.memset(RANK[:, :, :], 0.0))
                for a in range(NE):
                    for b in range(a + 1, NE):
                        step(nc.vector.tensor_tensor(GX[:, :], GL[:, :, b], GL[:, :, a], ALU.is_gt))
                        nc.vector.tensor_tensor(RANK[:, :, a], RANK[:, :, a], GX[:, :], ALU.add)
                        step(nc.vector.tensor_tensor(RANK[:, :, b], RANK[:, :, b], GX[:, :], ALU.subtract))
                        step(nc.vector.tensor_scalar(RANK[:, :, b], RANK[:, :, b], 1.0, None, ALU.add))
                step(nc.vector.tensor_scalar(RANK[:, :, :], RANK[:, :, :], 1.5, None, ALU.is_lt))
                nc.vector.tensor_tensor(keep["gates"][:, :].rearrange("p (e t) -> p t e", e=NE), GL[:, :, :], RANK[:, :, :], ALU.mult)

            dve.sem_inc(oh_free, BLK)
            done = dve.alloc_register("oh_blocks")
            dve.reg_mov(done, 0)
            with dve.Fori(0, NT) as w:
                lo = dve.value_load(blocks[0:1, 0, bass.ds(w, 1)], min_val=0, max_val=NB - 1)
                hi = dve.value_load(blocks[0:1, 1, bass.ds(w, 1)], min_val=1, max_val=NB)
                with dve.Fori(lo, hi) as b:
                    at = dve.snap(done, min_val=0, max_val=NT * NB)
                    for j in range(BLK):
                        dve.wait_ge(oh_free, at * BLK + j + 1)
                        nc.vector.tensor_scalar(ohs[0:EP, j, :], iota16[0:EP, :], srcF[:, bass.ds(b * BLK + j, 1)], None, ALU.is_equal)
                        nc.vector.tensor_scalar(ohd[0:EP, j, :], iota16[0:EP, bass.ds(w * P, P)], keep["dstF"][:, bass.ds(b * BLK + j, 1)], None, ALU.is_equal).then_inc(oh_ready, 1)
                    dve.reg_add(done, done, 1)
            dve.wait_ge(degrees_read, NT)
            step(nc.vector.tensor_reduce(maxdeg[:, :], degf, AX.X, ALU.max))
            nc.vector.tensor_scalar(large[:, :], maxdeg[:, :], EXACT, None, ALU.is_gt).then_inc(large_ready, 1)
            step(nc.vector.tensor_scalar(INV[:, :], degf, 1.0, None, ALU.max))
            step(nc.vector.reciprocal(INV[:, :], INV[:, :]))
            step(nc.vector.tensor_scalar(degf, degf, 1.0, None, ALU.min))
            step(nc.vector.tensor_tensor(INV[:, :], INV[:, :], degf, ALU.mult))
            logits()
            n = 0
            for t0, nt in SPANS:
                for k in range(KT):
                    dve.wait_ge(agg_ps, n + 1)
                    nc.vector.tensor_tensor(AGX[:, k, t0 * P:(t0 + nt) * P], ps[:, 4 + n % 4, 0:nt * P], INV[:, t0 * P:(t0 + nt) * P], ALU.mult).then_inc(agg_read, 1)
                    n += 1
                if t0 == 0:
                    gates()
            dve.sem_inc(dense_read, 2)
            dve.sem_inc(relu_done, 2)

            def normalized(i):
                t0, nt = SPANS[i]
                dve.wait_ge(y_added, (NE - 1) * NT + t0 + nt + 2)
                normalize(nc, dve, step, X, MID, t0, nt, (STATS, MV, RSTD), var_ready, std_ready, i, mid_ready)

            with dve.Fori(0, NE) as e:
                def biased(l, t):
                    dve.wait_ge(dense_ps, e * (2 * NT) + l * NT + t + 2)
                    if t == 0:
                        dve.wait_ge(bias_loaded, e * 32 + 16 * (l + 1))
                    dve.wait_ge(relu_done, e * (2 * NT) + l * NT + t + 1)
                    nc.vector.tensor_tensor(BIASED[:, t % 2, :], ps[:, t % 2, :], BB[:, l, :], ALU.add).then_inc(dense_read, 1)

                def low(t):
                    dve.wait_ge(relu_done, e * (2 * NT) + t + 3)
                    nc.vector.scalar_tensor_tensor(HL[:, t, :], BIASED[:, t % 2, :], 0.0, HH[:, t, :].bitcast(F32), ALU.max, ALU.subtract).then_inc(low_ready, 1)
                    dve.wait_ge(low_ready, e * NT + t + 2)

                for t in range(NT):
                    biased(0, t)
                    if t >= 1:
                        low(t - 1)
                low(NT - 1)
                n = 0
                for t0, nt in SPANS:
                    for k in range(KT):
                        dve.wait_ge(agg_ps, (e + 1) * (len(SPANS) * KT) + n + 1)
                        nc.vector.tensor_tensor(AG1[:, k, 0:nt * P], ps[:, 4 + n % 4, 0:nt * P], INV[:, t0 * P:(t0 + nt) * P], ALU.mult).then_inc(agg_read, 1)
                        n += 1
                    if t0 > 0:
                        with dve.If(e > NE - 2):
                            normalized(SPANS.index((t0, nt)) - 1)
                    for t in range(t0, t0 + nt):
                        biased(1, t)
            normalized(len(SPANS) - 1)

        @block.tensor
        def _(pe):
            pe.wait_ge(consts, 1)
            pe.wait_ge(ind_ready, 1)
            for b in range(4):
                mm = nc.tensor.matmul(ps[0:1, 4 + b, 0:400], ones16[0:EP, 0:1], ind.rearrange("p w k -> p (w k)")[:, b * 400:(b + 1) * 400], start=True, stop=True)
            mm.then_inc(counts_ps, 1)
            n = 0
            for i, (t0, nt) in enumerate(SPANS):
                pe.wait_ge(x_loaded[i], 32 if i == len(SPANS) - 1 else 16)
                for k in range(KT):
                    if n >= 2:
                        pe.wait_ge(tr_read, n - 1)
                    for t in range(nt):
                        mm = nc.tensor.transpose(ps[:, 2 + n % 2, t * P:(t + 1) * P], X[:, t0 + t, k * P:(k + 1) * P], ident[:, :])
                    mm.then_inc(tr_ps, 1)
                    n += 1
            pe.wait_ge(tr_read, n)
            pe.wait_ge(gate_loaded, 48)
            pe.wait_ge(counts_read, 1)
            for t in range(NT):
                for k in range(KT):
                    mm = nc.tensor.matmul(ps[:, 7, t * NE:(t + 1) * NE], XT[:, k, t * P:(t + 1) * P], GW[:, k, :], start=(k == 0), stop=(k == KT - 1))
            mm.then_inc(gate_ps, 1)
            pe.wait_ge(ranges_ready, 1)
            done = pe.alloc_register("oh_blocks_pe")
            pe.reg_mov(done, 0)
            def window(w, half):
                lo = pe.value_load(blocks[0:1, 0, bass.ds(w, 1)], min_val=0, max_val=NB - 1)
                hi = pe.value_load(blocks[0:1, 1, bass.ds(w, 1)], min_val=1, max_val=NB)
                pe.wait_ge(window_read, w + 1)
                for b, width in enumerate((4 * P, 4 * P, 3 * P)):
                    nc.tensor.matmul(ps[:, half * 4 + b, 0:width], zero16[:, :], iota16[:, 0:width].bitcast(BF16), start=True, stop=False)
                with pe.Fori(lo, hi) as blk:
                    at = pe.snap(done, min_val=0, max_val=NT * NB)
                    for j in range(BLK):
                        pe.wait_ge(oh_ready, at * BLK + j + 1)
                        for s in range(NT):
                            nc.tensor.matmul(ps[:, half * 4 + s // 4, (s % 4) * P:(s % 4 + 1) * P], ohs[0:EP, j, s * P:(s + 1) * P], ohd[0:EP, j, :], start=False, stop=False, skip_group_check=True)
                        nc.tensor.matmul(ps[:, half * 4 + 2, 2 * P:3 * P], ones16[0:EP, :], ohd[0:EP, j, :], start=False, stop=False, skip_group_check=True).then_inc(oh_free, 1)
                    pe.reg_add(done, done, 1)
                for b, width in enumerate((4 * P, 4 * P, 3 * P)):
                    mm = nc.tensor.matmul(ps[:, half * 4 + b, 0:width], zero16[:, :], iota16[:, 0:width].bitcast(BF16), start=False, stop=True)
                mm.then_inc(window_ps, 1)

            with pe.Fori(0, NT // 2) as turn:
                for half in range(2):
                    window(turn * 2 + half, half)
            pe.wait_ge(window_read, NT + 2)
            pe.sem_inc(left_used, 1)
            pe.sem_inc(dense_ps, 1)

            pe.wait_ge(large_ready, 1)
            beyond = pe.value_load(large[0:1, 0:1], min_val=0, max_val=1)

            def sum_rows(k, bank, t0, nt, counts, dt):
                for s in range(NT):
                    for part in (HH, HL):
                        mm = nc.tensor.matmul(ps[:, bank, 0:nt * P], part[:, s, k * P:(k + 1) * P].bitcast(dt), counts[:, s, t0 * P:(t0 + nt) * P], start=(s == 0 and part is HH), stop=(s == NT - 1 and part is HL))
                mm.then_inc(agg_ps, 1)

            def aggregate(t0, nt, n, before):
                for k in range(KT):
                    before(n + k)
                    with pe.If(beyond < 1):
                        sum_rows(k, 4 + (n + k) % 4, t0, nt, ATR, F32R)
                    with pe.If(beyond > 0):
                        sum_rows(k, 4 + (n + k) % 4, t0, nt, AT, F32)

            pe.wait_ge(low_ready, 1)
            n = 0
            for t0, nt in SPANS:
                aggregate(t0, nt, n, lambda m: pe.wait_ge(agg_read, m - 3) if m >= 4 else pe.wait_ge(logits_read, 1) if m == 3 else None)
                n += KT
            pe.wait_ge(agg_read, n)
            with pe.Fori(0, NE) as e:
                def transposed(t):
                    pe.wait_ge(tr_read, e * NT + len(SPANS) * KT + t - 1)
                    for k in range(KT):
                        for part in (HH, HL):
                            mm = nc.tensor.matmul(ps[:, 2 + t % 2, k * P:(k + 1) * P], part[:, t, k * P:(k + 1) * P], identr[:, :], start=(part is HH), stop=(part is HL))
                    mm.then_inc(tr_ps, 1)

                def dense(l, t, agg, own, a, own_ready=None):
                    for u in range(2):
                        pe.wait_ge(dense_read, e * (2 * NT) + l * NT + t + u + 1)
                        if t + u == 0:
                            pe.wait_ge(left_loaded, e * 32 + 16 * (l + 1))
                        for k in range(KT):
                            mm = nc.tensor.matmul(ps[:, u, :], agg[:, k, (a + u) * P:(a + u + 1) * P], WL[:, k, :], start=(k == 0), stop=False)
                    if t == NT - 2:
                        mm.then_inc(left_used, 1)
                    if t == 0:
                        pe.wait_ge(right_loaded, e * 32 + 16 * (l + 1))
                    if own_ready is not None:
                        pe.wait_ge(tr_read, own_ready)
                    for u in range(2):
                        for k in range(KT):
                            mm = nc.tensor.matmul(ps[:, u, :], own[:, k, (a + u) * P:(a + u + 1) * P], WR[:, k, :], start=False, stop=(k == KT - 1))
                        mm.then_inc(dense_ps, 1)

                for t in range(0, NT, 2):
                    dense(0, t, AGX, XT, t)
                pe.wait_ge(low_ready, e * NT + 3)
                for t in range(2):
                    transposed(t)
                pe.wait_ge(low_ready, (e + 1) * NT + 1)
                n = 0
                for t0, nt in SPANS:
                    aggregate(t0, nt, n, lambda m: pe.wait_ge(agg_read, (e + 1) * (len(SPANS) * KT) + m - 3))
                    n += KT
                    for t in range(max(t0, 2), t0 + nt):
                        transposed(t)
                    pe.wait_ge(agg_read, (e + 1) * (len(SPANS) * KT) + n)
                    for t in range(t0, t0 + nt, 2):
                        dense(1, t, AG1, H1T, t - t0, e * NT + len(SPANS) * KT + t0 + nt if t == t0 else None)


def messages_block(nc, dram, keep):
    ctx = ExitStack()
    with ctx:
        def sb(name, shape, dt=F32):
            return ctx.enter_context(nc.sbuf_tensor(name, shape, dt))

        def sem(name):
            return ctx.enter_context(nc.semaphore(name))

        SUM = sb("SUM", [P, NT, PATHS * EXT])
        X1 = sb("X1", [P, 2, G, D])
        X2 = [keep["x2"], sb("X2", [P, G, D])]
        PR = sb("PR", [P, 2, G, CW])
        DIF = keep["shared"][:, G * D:].bitcast(FP16).rearrange("p (a g n) -> p a g n", a=2, g=G)
        SQ = sb("SQ", [P, G, P], BF16)
        S = sb("S", [P, FIRST + OTHER, G, P])
        IDX = sb("IDX", [P, 2, G], I32)
        iota_f = sb("iota_f", [P, P])
        wbase = sb("wbase", [P, NT])
        zrow16 = sb("zrow16b", [P, CW], BF16)
        zero16 = zrow16[:, 0:P]
        sq = SQ[:, :, :].rearrange("p g n -> p (g n)")
        iota_i = sq.bitcast(I32)[:, 0:P]
        STATS = sq.bitcast(F32)[:, 0:6 * NT].rearrange("p (t s) -> p t s", s=6)
        MV = sq.bitcast(F32)[:, 6 * NT:8 * NT].rearrange("p (t s) -> p t s", s=2)
        RSTD = sq.bitcast(F32)[:, 8 * NT:9 * NT]
        HI = sb("HI", [P, SPLIT, CW], F32R)
        LO = sb("LO", [P, SPLIT, CW], F32R)
        ROW = X1[:, :, :, :].rearrange("p a g d -> p (a g) d")[:, 0:NT, :]
        OUT = PR[:, :, :, :].rearrange("p a g d -> p (a g) d")[:, 0:NT, :]
        ps = ctx.enter_context(nc.psum_tensor("psb", [P, 8, D], F32))

        x2_loaded = [keep["x2_loaded"], sem("x2_loaded1")]
        x1_loaded = [sem(f"x1_loaded{i}") for i in range(2)]
        idx_ready, waited, waited_v, waited_a, sum_zeroed = sem("idx_ready"), sem("waited"), sem("waited_v"), sem("waited_a"), sem("sum_zeroed")
        high_ready, low_ready = sem("high_readyb"), sem("low_readyb")
        first_zeroed = sem("first_zeroed")
        consts, iota_sem, zeroed = sem("constsb"), sem("iota_semb"), sem("zeroed")
        dif_ready, dif_used = sem("dif_ready"), sem("dif_used")
        products_ready = sem("products_ready")
        sq_done = sem("sq_done")
        onehot_ready, sums_ps, sums_read = sem("onehot_ready"), sem("sums_ps"), sem("sums_read")
        res_loaded, var_ready, std_ready, out_ready, out_stored = sem("res_loaded"), sem("var_readyb"), sem("std_readyb"), sem("out_ready"), sem("out_stored")
        chain_v = sem("chain_vb")
        block = ctx.enter_context(nc.Block())

        def windows_of(eng, regs, g):
            eng.load(regs, keep["windows"][0:1, bass.ds(g, 1), :].rearrange("p a k -> p (a k)"))

        def bounds(eng, regs):
            return eng.snap(regs[0], min_val=0, max_val=NT - 1), eng.snap(regs[1], min_val=1, max_val=NT)

        def groups(eng, body):
            with eng.Fori(0, NG // 2) as turn:
                for half in range(2):
                    body(turn * 2 + half, half, turn)

        @block.sync
        def _(sp):
            def load(g, half):
                sp.wait_ge(products_ready, (g + 1) * NC)
                sp.dma_start(X2[half][0:EP, :, :], dram["edge_attr"][bass.ds(g * (G * EP), G * EP), :].rearrange("(g p) d -> p g d", p=EP)).then_inc(x2_loaded[half], 16)
            sp.wait_ge(x1_loaded[0], 16 * G)
            load(1, 1)
            with sp.Fori(1, NG // 2) as turn:
                for half in range(2):
                    load(turn * 2 + half, half)
            for behind, tiles in ((NG + 1, slice(0, G)), (NG + 2, slice(G, NT))):
                sp.wait_ge(products_ready, behind * NC)
                sp.dma_start(ROW[:, tiles, :], dram["x_mid"].rearrange("(t p) d -> p t d", p=P)[:, tiles, :]).then_inc(res_loaded, 16)
            for i, (t0, nt) in enumerate(SPANS):
                sp.wait_ge(out_ready, i + 1)
                whole = min(nt, NT - 1 - t0)
                sp.dma_start(dram["out"][t0 * P:(t0 + whole) * P, :].rearrange("(t p) d -> p t d", p=P), OUT[:, t0:t0 + whole, :]).then_inc(out_stored, 16)
            sp.dma_start(dram["out"][(NT - 1) * P:N, :], OUT[0:LAST, NT - 1, :]).then_inc(out_stored, 16)
            sp.wait_ge(out_stored, 16 * (len(SPANS) + 1))

        @block.gpsimd
        def _(pool):
            def places(g, half):
                pool.wait_ge(dif_used, g + 1)
                ends = keep["dstF"][:, bass.ds(g * G, G)]
                nc.gpsimd.tensor_tensor(DIF[0:EP, half, :, :], iota_f[0:EP, :].unsqueeze(1).broadcast_to([EP, G, P]), ends.unsqueeze(2).broadcast_to([EP, G, P]), ALU.subtract).then_inc(dif_ready, 1)

            def indices(g, half):
                pool.wait_ge(products_ready, (g + 1) * NC)
                nc.gpsimd.tensor_copy(IDX[0:EP, half, :], keep["src"][:, bass.ds(g * G, G)]).then_inc(idx_ready, 1)
                pool.wait_ge(idx_ready, g + 1)
                pool.sem_inc(waited, 1)

            def gather(half, tiles):
                for j in tiles:
                    nc.gpsimd.indirect_dma_start(out=X1[0:EP, half, j, :], out_offset=None, in_=dram["x_mid"],
                                                 in_offset=bass.IndirectOffsetOnAxis(ap=IDX[0:EP, half, j:j + 1], axis=0)).then_inc(x1_loaded[half], 16)

            def group(g, half, following):
                if following:
                    indices(g + 1, 1 - half)
                    gather(1 - half, range(0, 2))
                    places(g + 1, 1 - half)
                for c in range(NC):
                    pool.wait_ge(high_ready, g * NC + c + 1)
                    nc.gpsimd.tensor_tensor(LO[0:EP, :, :], PR[0:EP, c % 2, G - SPLIT:G, :], HI[0:EP, :, :].bitcast(F32), ALU.subtract).then_inc(low_ready, 1)
                    if following and c < 2:
                        gather(1 - half, range(2 + 3 * c, 5 + 3 * c))

            indices(0, 0)
            gather(0, range(G))
            nc.gpsimd.iota(iota_i[:, :], [[1, P]], base=0, channel_multiplier=0).then_inc(iota_sem, 1)
            pool.wait_ge(iota_sem, 1)
            nc.gpsimd.tensor_copy(iota_f[:, :], iota_i[:, :]).then_inc(consts, 1)
            pool.wait_ge(consts, 1)
            places(0, 0)
            nc.gpsimd.memset(SUM[:, ZA:NT, :], 0.0).then_inc(sum_zeroed, 1)
            with pool.Fori(0, NG // 2 - 1) as turn:
                for half in range(2):
                    group(turn * 2 + half, half, True)
            group(NG - 2, 0, True)
            group(NG - 1, 1, False)

        @block.vector
        def _(dve):
            step = Chain(dve, chain_v)
            for credit in (dif_used, sums_read, sums_ps, low_ready):
                dve.sem_inc(credit, 2)
            dve.sem_inc(products_ready, 2 * NC)
            nc.vector.memset(SUM[:, 0, :], 0.0).then_inc(first_zeroed, 1)
            for w in range(NT):
                nc.vector.memset(wbase[:, w:w + 1], float(w * P))
            step(nc.vector.memset(zrow16[:, :], 0.0))
            dve.sem_inc(zeroed, 1)
            nc.vector.memset(SUM[:, 1:ZV, :], 0.0).then_inc(sum_zeroed, 1)
            pairs = dve.alloc_register("pairs_v")
            span = [dve.alloc_register(f"span_v{i}") for i in range(2)]
            ahead = [dve.alloc_register(f"ahead_v{i}") for i in range(2)]
            windows_of(dve, span, 0)
            dve.reg_mov(pairs, 0)

            def next_windows():
                for r, q in zip(span, ahead):
                    dve.reg_mov(r, q)

            def add_sums(c):
                lo, hi = bounds(dve, span)
                with dve.Fori(lo, hi) as w:
                    at = dve.snap(pairs, min_val=0, max_val=NT * NG * NC)
                    dve.wait_ge(sums_ps, at + 3)
                    acc = SUM[:, bass.ds(w, 1), c * CW:(c + 1) * CW]
                    nc.vector.tensor_tensor(acc, acc, ps[:, bass.ds((w % 2) * NC + c, 1), :], ALU.add).then_inc(sums_read, 1)
                    dve.reg_add(pairs, pairs, 1)

            def load_paths(c):
                regs = [dve.alloc_register(f"path_off{next(made)}") for _ in range(2 * PC)]
                dve.load(regs, keep["path"][0:1, c * 2 * PC:(c + 1) * 2 * PC])
                return [dve.snap(r, True, min_val=0, max_val=D - EXT) for r in regs]

            paths, made = [None], count()

            def products(g, half, turn):
                if half == 0:
                    paths[0] = load_paths(0)
                for c in range(NC):
                    off = paths[0]
                    if c == 0:
                        dve.wait_ge(x1_loaded[half], turn * (16 * G) + 16 * G)
                        dve.wait_ge(x2_loaded[half], turn * 16 + 16)
                    for j in range(PC):
                        ins = nc.vector.tensor_tensor(PR[0:EP, c % 2, :, j * EXT:(j + 1) * EXT], X1[0:EP, half, :, bass.ds(off[j], EXT)], X2[half][0:EP, :, bass.ds(off[PC + j], EXT)], ALU.mult)
                    ins.then_inc(products_ready, 1)
                    if (half, c) != (1, NC - 1):
                        paths[0] = load_paths((c + 1) % NC)
                    if c == 0:
                        windows_of(dve, ahead, g)
                    dve.wait_ge(low_ready, g * NC + c + 2)
                    dve.sem_inc(waited_v, 1)
                    if c >= 1:
                        add_sums(c - 1)
                    elif half:
                        add_sums(NC - 1)
                        next_windows()
                    else:
                        with dve.If(turn > 0):
                            add_sums(NC - 1)
                        with dve.If(turn < 1):
                            dve.wait_ge(sum_zeroed, 3)
                            dve.sem_inc(waited_v, 1)
                        next_windows()

            groups(dve, products)
            dve.wait_ge(res_loaded, 32)
            for c in range(PATHS // (2 * PC)):
                if c == PATHS // (2 * PC) - 1:
                    add_sums(NC - 1)
                regs = [dve.alloc_register(f"seg_off{c}_{i}") for i in range(2 * PC)]
                dve.load(regs, keep["path"][0:1, 2 * PATHS + c * 2 * PC:2 * PATHS + (c + 1) * 2 * PC])
                off = [dve.snap(r, True, min_val=0, max_val=D - EXT) for r in regs]
                for j in range(2 * PC):
                    p = c * 2 * PC + j
                    for half in (slice(0, NT // 2), slice(NT // 2, NT)):
                        seg = ROW[:, half, bass.ds(off[j], EXT)]
                        step(nc.vector.scalar_tensor_tensor(seg, SUM[:, half, p * EXT:(p + 1) * EXT], keep["coef"][:, p:p + 1], seg, ALU.mult, ALU.add), running=1)
            step(nc.vector.memset(RSTD[:, 0:1], 0.0))
            for i, (t0, nt) in enumerate(SPANS):
                normalize(nc, dve, step, ROW, OUT, t0, nt, (STATS, MV, RSTD), var_ready, std_ready, i, out_ready)

        @block.scalar
        def _(act):
            made, before, second = (act.alloc_register(name) for name in ("pairs_a", "pairs_before", "second_window"))
            span = [act.alloc_register(f"span_a{i}") for i in range(2)]
            act.reg_mov(made, 0)
            act.sem_inc(onehot_ready, 1)
            act.wait_ge(zeroed, 1)
            act.wait_ge(first_zeroed, 1)
            for w in range(ZV, ZA):
                nc.scalar.copy(SUM[:, w, :], SUM[:, 0, :])
            act.drain().then_inc(sum_zeroed, 1)

            def onehots(g, half, turn):
                act.wait_ge(dif_ready, g + 1)
                windows_of(act, span, g)
                lo, hi = bounds(act, span)

                def onehot(w, slot, used=None):
                    at = act.snap(made, min_val=0, max_val=NT * NG * NC)
                    act.wait_ge(onehot_ready, at + 1)
                    act.sem_inc(waited_a, 1)
                    nc.scalar.activation(SQ[0:EP, :, :], DIF[0:EP, half, :, :], ACT.Square, bias=wbase[0:EP, bass.ds(w, 1)]).then_inc(sq_done, 1)
                    act.wait_ge(sq_done, at + 1)
                    if used is not None:
                        act.wait_ge(sums_ps, at + 2 - used)
                    nc.scalar.activation(S[0:EP, slot, :, :].bitcast(F32R), SQ[0:EP, :, :], ACT.Relu, bias=1.0, scale=-1.0).then_inc(onehot_ready, 1)
                    act.reg_add(made, made, 1)

                for c in range(NC):
                    act.reg_mov(before, made)
                    onehot(lo, c % FIRST)
                    with act.If(hi - lo > 1):
                        act.reg_add(second, span[0], 1)
                        onehot(act.snap(second, min_val=1, max_val=NT - 1), FIRST, 1)
                    act.wait_ge(products_ready, (g + 2) * NC + c + 1)
                    act.wait_ge(sums_ps, act.snap(before, min_val=0, max_val=NT * NG * NC) + 2)
                    act.wait_ge(low_ready, g * NC + c + 2)
                    nc.scalar.copy(HI[0:EP, :, :], PR[0:EP, c % 2, G - SPLIT:G, :]).then_inc(high_ready, 1)
                    with act.If(hi - lo > 2):
                        with act.Fori(lo + 2, hi) as w:
                            onehot(w, FIRST, 0)
                act.drain().then_inc(dif_used, 1)
            groups(act, onehots)
            for i, (t0, nt) in enumerate(SPANS):
                act.wait_ge(var_ready, i + 1)
                nc.scalar.activation(RSTD[:, t0:t0 + nt], RSTD[:, t0:t0 + nt], ACT.Sqrt).then_inc(std_ready, 1)

        @block.tensor
        def _(pe):
            pe.wait_ge(zeroed, 1)
            pairs = pe.alloc_register("pairs_t")
            span = [pe.alloc_register(f"span_t{i}") for i in range(2)]
            flags = [pe.alloc_register(f"here{j}") for j in range(G)]
            pe.reg_mov(pairs, 0)

            def window(g, c, w, slot):
                pe.load(flags, keep["present"][0:1, bass.ds(w, 1), bass.ds(g * G, G)].rearrange("p a k -> p (a k)"))
                here = [pe.snap(r, min_val=0, max_val=1) for r in flags]
                at = pe.snap(pairs, min_val=0, max_val=NT * NG * NC)
                bank = ps[:, bass.ds((w % 2) * NC + c, 1), :].rearrange("p a n -> p (a n)")
                pe.wait_ge(products_ready, (g + 2) * NC + c + 1)
                pe.wait_ge(onehot_ready, at + 2)
                pe.wait_ge(sums_read, at + 1)
                nc.tensor.matmul(bank, zero16[0:EP, :], zrow16[0:EP, :], start=True, stop=True)
                for first in range(0, G, G // 2):
                    tiles = range(first, first + G // 2)
                    with pe.If(pe.snap(sum(here[j] for j in tiles), min_val=0, max_val=G // 2) > 0):
                        for j in tiles:
                            with pe.If(here[j] > 0):
                                onehot, rows = S[0:EP, slot, j, :], PR[0:EP, c % 2, j, :]
                                if j < G - SPLIT:
                                    nc.tensor.matmul(bank, onehot, rows, start=False, stop=True, skip_group_check=True)
                                else:
                                    pe.wait_ge(low_ready, g * NC + c + 3)
                                    for part in (HI[0:EP, j - (G - SPLIT), :], LO[0:EP, j - (G - SPLIT), :]):
                                        nc.tensor.matmul(bank, onehot.bitcast(F32R), part, start=False, stop=True, skip_group_check=True)
                nc.tensor.matmul(bank[:, 0:1], zero16[0:EP, :], zrow16[0:EP, 0:1], start=False, stop=True, skip_group_check=True).then_inc(sums_ps, 1)
                pe.reg_add(pairs, pairs, 1)

            def sums(g, half, turn):
                windows_of(pe, span, g)
                lo, hi = bounds(pe, span)
                for c in range(NC):
                    window(g, c, lo, c % FIRST)
                    with pe.If(hi - lo > 1):
                        with pe.Fori(lo + 1, hi) as w:
                            window(g, c, w, FIRST)
            groups(pe, sums)


def gnn_kernel(nc, x, srcT, dstT, edge_attr, gate_W, gate_b, Wl, bl, Wr, coeffs, paths, out):
    ctx = ExitStack()
    with ctx:
        x_mid = nc.dram_tensor("x_mid", (NP, D), F32, kind="Internal").ap()
        dram = dict(x=x, srcT=srcT, dstT=dstT, edge_attr=edge_attr, gate_W=gate_W, gate_b=gate_b,
                    Wl=Wl, bl=bl, Wr=Wr, coeffs=coeffs, paths=paths, out=out, x_mid=x_mid)
        keep = {}
        for name, shape, dt in (("src", [EP, ET], I32),
                                ("dstF", [EP, ET], F32), ("path", [1, 3 * PATHS], I32), ("coef", [P, PATHS], F32),
                                ("gates", [P, NE * NT], F32), ("present", [1, NT, ET], mybir.dt.uint8),
                                ("windows", [1, NG, 2], I32)):
            keep[name] = ctx.enter_context(nc.sbuf_tensor(name + "_kept", shape, dt))
        keep["shared"] = ctx.enter_context(nc.sbuf_tensor("shared_kept", [P, KT * NP], F32))
        keep["x2"] = keep["shared"][:, 0:G * D].rearrange("p (g d) -> p g d", d=D)
        keep["x2_loaded"] = ctx.enter_context(nc.semaphore("x2_loaded0"))
        experts_block(nc, dram, keep)
        messages_block(nc, dram, keep)


def kernel(x, src, dst, edge_attr_512, L0_gnn_gate_W, L0_gnn_gate_b, L0_gnn_Wl, L0_gnn_bl, L0_gnn_Wr,
           L1_gnn_path_coeffs, L1_gnn_path_indices):
    import numpy as np
    import concourse.bacc as bacc
    from concourse.bass_utils import run_bass_kernel_spmd

    c = np.ascontiguousarray
    paths = np.asarray(L1_gnn_path_indices)
    arrays = {
        "x": c(x),
        "srcT": c(np.asarray(src).reshape(ET, EP).T),
        "dstT": c(np.asarray(dst).reshape(ET, EP).T),
        "edge_attr": c(edge_attr_512),
        "gate_W": c(L0_gnn_gate_W), "gate_b": c(L0_gnn_gate_b),
        "Wl": c(L0_gnn_Wl), "bl": c(L0_gnn_bl), "Wr": c(L0_gnn_Wr),
        "coeffs": c(L1_gnn_path_coeffs),
        "paths": np.concatenate([c(paths[:, 0:2].reshape(NC, PC, 2).transpose(0, 2, 1)).reshape(-1), paths[:, 2]]),
    }
    nc = bacc.Bacc("TRN2", target_bir_lowering=False, num_devices=1)
    args = [nc.dram_tensor(f"in_{k}", a.shape, mybir.dt.from_np(a.dtype), kind="ExternalInput").ap() for k, a in arrays.items()]
    out = nc.dram_tensor("out_dram", (N, D), F32, kind="ExternalOutput").ap()
    gnn_kernel(nc, *args, out)
    r = run_bass_kernel_spmd(nc, [{f"in_{k}": a for k, a in arrays.items()}], core_ids=[0])
    return r.results[0]["out_dram"]
```
